# Optimizing a Trainium2 kernel written in Bass

```python
import numpy as np
import jax
import jax.numpy as jnp

def _softmax(x, axis=-1):
    return jax.nn.softmax(x, axis=axis)

def _gelu(x):
    return jax.nn.gelu(x, approximate=True)

def _silu(x):
    return jax.nn.silu(x)

def _sigmoid(x):
    return jax.nn.sigmoid(x)

def _layernorm(x, axis=-1, eps=1e-05):
    m = jnp.mean(x, axis=axis, keepdims=True)
    v = jnp.var(x, axis=axis, keepdims=True)
    return (x - m) / jnp.sqrt(v + eps)

def _scatter_add(tgt, idx, src, axis=0):
    return tgt.at[idx].add(src)

def _segment_sum(src, seg, n):
    return jax.ops.segment_sum(src, seg, n)
kernel_name = 'mk_seq_preln_d1_jaxref_r4_83dd5b'

def setup_inputs(seed: int=0):
    np.random.seed(seed)
    _w = jnp.asarray

    def _L0_attn_setup():
        import jax, jax.numpy as jnp
        import numpy as np
        import math
        B, T, D = (2, 512, 512)
        H, G, DQ, DV = (16, 4, 128, 128)
        REP = H // G
        ROPE_THETA = 10000.0

        def _rope(x):
            t = x.shape[2]
            inv_freq = 1.0 / ROPE_THETA ** (jnp.arange(0, DQ, 2, dtype=jnp.float32) / DQ)
            freqs = jnp.arange(t, dtype=jnp.float32)[:, None] * inv_freq[None, :]
            freqs = jnp.repeat(freqs, 2, axis=-1)
            cos, sin = (jnp.cos(freqs), jnp.sin(freqs))
            x2 = x.reshape(*x.shape[:-1], DQ // 2, 2)
            rot = jnp.stack([-x2[..., 1], x2[..., 0]], axis=-1).reshape(x.shape)
            return x * cos + rot * sin

        def _alibi(t):
            slopes = 2.0 ** (-jnp.arange(1, H + 1, dtype=jnp.float32) * 8.0 / H)
            pos = jnp.arange(t, dtype=jnp.float32)
            diff = jnp.abs(pos[:, None] - pos[None, :])
            return -diff[None, :, :] * slopes[:, None, None]
        key = jax.random.key(seed)
        ks = jax.random.split(key, 5)
        s = 0.02
        return {'hidden_states': jax.random.normal(ks[0], (B, T, D), jnp.float32), 'Wq': jax.random.normal(ks[1], (D, H * DQ), jnp.float32) * s, 'Wk': jax.random.normal(ks[2], (D, G * DQ), jnp.float32) * s, 'Wv': jax.random.normal(ks[3], (D, G * DV), jnp.float32) * s, 'Wo': jax.random.normal(ks[4], (H * DV, D), jnp.float32) * s, 'bo': jnp.zeros((D,), jnp.float32)}
    _L0_attn_in = _L0_attn_setup()

    def _L0_ffn_setup():
        import jax, jax.numpy as jnp
        import numpy as np
        B, S, D_IN, D_OUT, E = (4, 256, 512, 512, 32)
        MASK_DENSITY = 0.3
        THRESH = 0.5
        key = jax.random.key(seed)
        k_x, k_w, k_m, k_r = jax.random.split(key, 4)
        x = jax.random.normal(k_x, (B, S, D_IN), dtype=jnp.float32)
        bound = np.sqrt(1.0 / D_IN) * np.sqrt(3.0)
        weight = jax.random.uniform(k_w, (D_OUT, D_IN), minval=-bound, maxval=bound, dtype=jnp.float32)
        scale = jnp.ones((D_OUT,), dtype=jnp.float32)
        expert_masks = (jax.random.uniform(k_m, (E, D_OUT, D_IN)) < MASK_DENSITY).astype(jnp.float32)
        router_w = 0.01 * jax.random.normal(k_r, (E, D_IN), dtype=jnp.float32)
        return {'x': x, 'weight': weight, 'scale': scale, 'expert_masks': expert_masks, 'router_w': router_w}
    _L0_ffn_in = _L0_ffn_setup()
    _d = {'L0_attn_hidden_states': _L0_attn_in['hidden_states'], 'L0_attn_Wq': _L0_attn_in['Wq'], 'L0_attn_Wk': _L0_attn_in['Wk'], 'L0_attn_Wv': _L0_attn_in['Wv'], 'L0_attn_Wo': _L0_attn_in['Wo'], 'L0_attn_bo': _L0_attn_in['bo'], 'L0_ffn_weight': _L0_ffn_in['weight'], 'L0_ffn_scale': _L0_ffn_in['scale'], 'L0_ffn_expert_masks': _L0_ffn_in['expert_masks'], 'L0_ffn_router_w': _L0_ffn_in['router_w']}
    _x0 = _d['L0_attn_hidden_states']
    _d['L0_attn_hidden_states'] = jax.random.normal(jax.random.fold_in(jax.random.key(seed), 1), (2, 1024, 512), dtype=_x0.dtype)
    del _x0
    return _d

def reference(L0_attn_hidden_states, L0_attn_Wq, L0_attn_Wk, L0_attn_Wv, L0_attn_Wo, L0_attn_bo, L0_ffn_weight, L0_ffn_scale, L0_ffn_expert_masks, L0_ffn_router_w):

    def _L0_attn_ref(hidden_states, Wq, Wk, Wv, Wo, bo):
        import jax, jax.numpy as jnp
        import numpy as np
        import math
        B, T, D = (2, 512, 512)
        H, G, DQ, DV = (16, 4, 128, 128)
        REP = H // G
        ROPE_THETA = 10000.0

        def _rope(x):
            t = x.shape[2]
            inv_freq = 1.0 / ROPE_THETA ** (jnp.arange(0, DQ, 2, dtype=jnp.float32) / DQ)
            freqs = jnp.arange(t, dtype=jnp.float32)[:, None] * inv_freq[None, :]
            freqs = jnp.repeat(freqs, 2, axis=-1)
            cos, sin = (jnp.cos(freqs), jnp.sin(freqs))
            x2 = x.reshape(*x.shape[:-1], DQ // 2, 2)
            rot = jnp.stack([-x2[..., 1], x2[..., 0]], axis=-1).reshape(x.shape)
            return x * cos + rot * sin

        def _alibi(t):
            slopes = 2.0 ** (-jnp.arange(1, H + 1, dtype=jnp.float32) * 8.0 / H)
            pos = jnp.arange(t, dtype=jnp.float32)
            diff = jnp.abs(pos[:, None] - pos[None, :])
            return -diff[None, :, :] * slopes[:, None, None]
        N, t, _ = hidden_states.shape
        q = (hidden_states @ Wq).reshape(N, t, H, DQ).transpose(0, 2, 1, 3)
        k = (hidden_states @ Wk).reshape(N, t, G, DQ).transpose(0, 2, 1, 3)
        v = (hidden_states @ Wv).reshape(N, t, G, DV).transpose(0, 2, 1, 3)
        q = _rope(q)
        k = _rope(k)
        k = jnp.repeat(k, REP, axis=1)
        v = jnp.repeat(v, REP, axis=1)
        scores = jnp.einsum('bhtd,bhsd->bhts', q, k)
        scores = scores + _alibi(t)[None]
        scores = scores / math.sqrt(DQ)
        scores = 30.0 * jnp.tanh(scores / 30.0)
        causal = jnp.tril(jnp.ones((t, t), bool))
        scores = jnp.where(causal[None, None], scores, -jnp.inf)
        probs = jax.nn.softmax(scores, axis=-1)
        ctx = jnp.einsum('bhts,bhsd->bhtd', probs, v)
        ctx = ctx.transpose(0, 2, 1, 3).reshape(N, t, H * DV)
        return ctx @ Wo + bo

    def _L0_ffn_ref(x, weight, scale, expert_masks, router_w):
        import jax, jax.numpy as jnp
        import numpy as np
        B, S, D_IN, D_OUT, E = (4, 256, 512, 512, 32)
        MASK_DENSITY = 0.3
        THRESH = 0.5
        logits = jnp.einsum('bsd,ed->bse', x, router_w)
        probs = jax.nn.softmax(logits, axis=-1)
        top1_w = jnp.max(probs, axis=-1)
        top1_idx = jnp.argmax(probs, axis=-1)
        w_q = jnp.clip(jnp.round(weight / THRESH), -1.0, 1.0)
        w_scaled = w_q * scale[:, None]
        out0 = jnp.zeros((x.shape[0], x.shape[1], weight.shape[0]), dtype=x.dtype)

        def body(out, inputs):
            e_idx, mask_e = inputs
            y = jnp.einsum('bsi,oi->bso', x, w_scaled * mask_e)
            sel = (top1_idx == e_idx)[..., None]
            out = jnp.where(sel, y * top1_w[..., None], out)
            return (out, None)
        out, _ = jax.lax.scan(body, out0, (jnp.arange(E), expert_masks))
        return out
    x = L0_attn_hidden_states
    x = x + _L0_attn_ref(_layernorm(x, axis=-1), L0_attn_Wq, L0_attn_Wk, L0_attn_Wv, L0_attn_Wo, L0_attn_bo)
    x = x + _L0_ffn_ref(_layernorm(x, axis=-1), L0_ffn_weight, L0_ffn_scale, L0_ffn_expert_masks, L0_ffn_router_w)
    return x

_drawn_inputs = setup_inputs


def setup_inputs(seed=0):
    import zlib

    import numpy as np

    out = dict(_drawn_inputs(seed))
    spreads = {'L0_attn_bo': (0.0, 0.1), 'L0_ffn_scale': (1.0, 0.2)}
    factors = {'L0_attn_Wq': 6.291, 'L0_attn_Wk': 6.304}
    for name, (base, spread) in spreads.items():
        noise = np.random.default_rng([zlib.crc32(name.encode()), seed]).standard_normal(out[name].shape)
        drawn = base * np.exp(spread * noise) if base else spread * noise
        out[name] = jnp.asarray(drawn.astype(out[name].dtype))
    for name, factor in factors.items():
        out[name] = (out[name] * factor).astype(out[name].dtype)
    return out
```

```python
from contextlib import ExitStack

import numpy as np

import concourse.bass as bass
from concourse import mybir

ALU = mybir.AluOpType
ACT = mybir.ActivationFunctionType
AX = mybir.AxisListType
F32 = mybir.dt.float32
F32R = mybir.dt.float32r
I32 = mybir.dt.int32
U32 = mybir.dt.uint32

P = 128
B, T, D = 2, 1024, 512
H, G, DH = 16, 4, 128
REP = H // G
E = 32
NT = T // P
TILES = B * NT
DC = D // P
QC = T // 512
LN_EPS = 1e-5
ROPE_THETA = 10000.0
TANH_CAP = 30.0
SLOT_TILES = TILES + E
NO_TOKEN = 2 * B * T
ROUND = 1.5 * 2.0 ** 23

UNITS = [
    [(0, 0, 0, 512, 0), (1, 0, 128, 384, 512), (3, 0, 384, 128, 896)],
    [(2, 0, 256, 256, 0), (6, 1, 256, 256, 256)],
    [(1, 1, 0, 512, 0), (0, 1, 0, 512, 512)],
    [(3, 1, 0, 512, 0), (2, 1, 0, 512, 512)],
    [(4, 1, 0, 512, 0), (5, 1, 128, 384, 512), (7, 1, 384, 128, 896)],
]
NU = len(UNITS)
WIDTH = [sum(e[3] for e in u) for u in UNITS]
DIAGONAL = [True, True, False, False, True]
ADDS = 11
ADD_RANK = [3, 6, 5, 8, 11]
MASKS = 3
MASK_RANK = [1, 2, None, None, 3]
UNITS_IT = REP * NU
P_SLOTS = 3
ROPES_IT = 2 * REP + 2
OUTS_IT = REP * NT
LN_STEPS = 2 * NT + 5
CONSTS = 7
CONSTS2 = 8
SHIFTED, HOT_KNOWN, SLOTS_KNOWN, EXPERTS_KNOWN = 2, 7, 36, 39


def bank_jobs():
    jobs = [("rope", n) for n in range(4)] + [("vproj", 0), ("vproj", 1), ("vturn", 0), ("vturn", 1)]
    rope = 4
    for r in range(REP):
        if r:
            jobs += [("sum", r - 1)] + [("out", (r - 1) * NT + t) for t in range(NT)]
        if r < REP - 1:
            jobs += [("rope", rope), ("rope", rope + 1)]
            rope += 2
    jobs += [("sum", REP - 1)] + [("out", (REP - 1) * NT + t) for t in range(NT)]
    return jobs


JOBS = bank_jobs()
assert len(JOBS) % 2 == 0


def block_kernel(nc, x, wq, wkv, wo, bo, cosines, sines, negslopes, reach_near, reach_far, ident_in, earlier_in,
                 expert_ids_in, tile_ids_in, token_ids_in, no_tokens_in, past_end_in, router, weight, scale,
                 masks, rows_d, slot_tokens_d, out):
    ctx = ExitStack()
    with ctx:
        attn = ExitStack()

        def sb(name, shape, dt=F32, stack=ctx):
            return stack.enter_context(nc.sbuf_tensor(name, shape, dt))

        def asb(name, shape, dt=F32):
            return sb(name, shape, dt, attn)

        def sem(name):
            return ctx.enter_context(nc.semaphore(name))

        acc = sb("acc", [P, TILES, D])
        ident = sb("ident", [P, P])
        ones = sb("ones", [P, P])
        mean_var = sb("mean_var", [P, TILES, 2])
        stats = sb("stats", [P, TILES, 6])
        rs = sb("rs", [P, 4, TILES])
        xnorm = sb("xnorm", [P, 2, D])

        xt_hi = asb("xt_hi", [P, DC, T], F32R)
        xt_lo = asb("xt_lo", [P, DC, T], F32R)
        k_hi = asb("k_hi", [P, T], F32R)
        k_lo = asb("k_lo", [P, T], F32R)
        v_rows = asb("v_rows", [P, T])
        v_hi = asb("v_hi", [P, NT, DH], F32R)
        v_lo = asb("v_lo", [P, NT, DH], F32R)
        q_hi = asb("q_hi", [P, 2, T], F32R)
        q_lo = asb("q_lo", [P, 2, T], F32R)
        probs = asb("probs", [P, P_SLOTS, 1024])
        p_hi = asb("p_hi", [P, P_SLOTS, 1024], F32R)
        p_lo = asb("p_lo", [P, P_SLOTS, 1024], F32R)
        psums = asb("psums", [P, T])
        ctx_hi = asb("ctx_hi", [P, T], F32R)
        ctx_lo = asb("ctx_lo", [P, T], F32R)
        rinv = asb("rinv", [P, NT])
        wq_in = asb("wq_in", [P, DC * DH])
        wq_hi = asb("wq_hi", [P, DC, DH], F32R)
        wq_lo = asb("wq_lo", [P, DC, DH], F32R)
        wo_in = asb("wo_in", [P, D])
        wo_hi = asb("wo_hi", [P, D], F32R)
        wo_lo = asb("wo_lo", [P, D], F32R)
        wkv_in = asb("wkv_in", [P, 2 * DC * DH])
        wkv_hi = asb("wkv_hi", [P, 2, DC, DH], F32R)
        wkv_lo = asb("wkv_lo", [P, 2, DC, DH], F32R)
        cos_t = asb("cos_t", [P, T])
        sin_t = asb("sin_t", [P, T])
        rope_a = asb("rope_a", [P, 2, 512])
        rope_b = asb("rope_b", [P, 2, 512])
        bo_t = asb("bo_t", [P, D])
        slopes = asb("slopes", [P, H])
        far = asb("far", [P, 7 * P])
        near = asb("near", [P, 1024])
        attn.close()

        xn = sb("xn", [P, TILES, D])
        xn_t = sb("xn_t", [P, 2, D])
        router_t = sb("router_t", [P, DC, E])
        logits = sb("logits", [P, TILES, E])
        expo = sb("expo", [P, TILES, E])
        top = sb("top", [P, TILES])
        first = sb("first", [P, TILES])
        top_w = sb("top_w", [P, 2, TILES])
        expert_ids = sb("expert_ids", [P, TILES, E])
        one_hot = sb("one_hot", [P, TILES, E])
        rank = sb("rank", [P, TILES, E])
        before = sb("before", [P, TILES + 1, E])
        earlier = sb("earlier", [P, P])
        expert_tiles = sb("expert_tiles", [P, 4, E])
        expert_tiles_i = sb("expert_tiles_i", [P, 2, E], I32)
        slot_f = sb("slot_f", [P, TILES])
        slot_i = sb("slot_i", [P, TILES], U32)
        token_ids = sb("token_ids", [P, TILES])
        tile_ids = sb("tile_ids", [1, SLOT_TILES, E])
        tile_past = sb("tile_past", [1, SLOT_TILES, E])
        tile_expert = sb("tile_expert", [1, SLOT_TILES])
        tile_expert_i = sb("tile_expert_i", [1, SLOT_TILES], I32)
        slot_tok = sb("slot_tok", [SLOT_TILES, P])
        slot_tok_i = sb("slot_tok_i", [P, SLOT_TILES + 2], U32)
        weight_t = sb("weight_t", [P, DC * D])
        scale_t = sb("scale_t", [P, D])
        mask = sb("mask", [P, 2, DC * D])
        w_exp = sb("w_exp", [P, 2, DC, D])
        row = [sb(f"row{i}", [P, 2 * D]) for i in range(2)]
        row_t = sb("row_t", [P, 2, D])
        row_idx = [sb(f"row_idx{i}", [P, 1], U32) for i in range(2)]
        out_idx = [sb(f"out_idx{i}", [P, 1], U32) for i in range(2)]
        y = [sb(f"y{i}", [P, D]) for i in range(2)]

        score_ps = ctx.enter_context(nc.psum_tensor("score_ps", [P, 2, 1024], F32))
        ctx_ps = ctx.enter_context(nc.psum_tensor("ctx_ps", [P, 2, 512], F32))
        work = ctx.enter_context(nc.psum_tensor("work", [P, 2, 512], F32))

        consts_in = sem("consts_in")
        x_in = sem("x_in")
        wq_landed, wo_landed, wkv_landed = sem("wq_landed"), sem("wo_landed"), sem("wkv_landed")
        wq_split_hi, wq_split_lo = sem("wq_split_hi"), sem("wq_split_lo")
        wo_split_hi, wo_split_lo = sem("wo_split_hi"), sem("wo_split_lo")
        wkv_split_hi, wkv_split_lo = sem("wkv_split_hi"), sem("wkv_split_lo")
        ones_set = sem("ones_set")
        ln_step, ln_root, ln_normed = sem("ln_step"), sem("ln_root"), sem("ln_normed")
        ln_turned, ln_hi, ln_lo = sem("ln_turned"), sem("ln_hi"), sem("ln_lo")
        bias_added = sem("bias_added")
        projected = sem("projected")
        rope_ready, rope_sum, rope_hi, rope_lo = sem("rope_ready"), sem("rope_sum"), sem("rope_hi"), sem("rope_lo")
        v_projected, v_copied = sem("v_projected"), sem("v_copied")
        v_turned, v_split_hi, v_split_lo = sem("v_turned"), sem("v_split_hi"), sem("v_split_lo")
        scored, biased, tanhed, exped, masked = (sem("scored"), sem("biased"), sem("tanhed"), sem("exped"),
                                                 sem("masked"))
        p_split_hi, p_split_lo, p_added = sem("p_split_hi"), sem("p_split_lo"), sem("p_added")
        pv_done = sem("pv_done")
        ctx_split_hi, ctx_split_lo = sem("ctx_split_hi"), sem("ctx_split_lo")
        summed, inverted = sem("summed"), sem("inverted")
        out_done, out_added = sem("out_done"), sem("out_added")
        consts2_in = sem("consts2_in")
        l2_step, l2_root, l2_normed = sem("l2_step"), sem("l2_root"), sem("l2_normed")
        l2_turned, l2_copied = sem("l2_turned"), sem("l2_copied")
        l2_logits, l2_kept = sem("l2_logits"), sem("l2_kept")
        route, route_exp, ranked = sem("route"), sem("route_exp"), sem("ranked")
        x1_rows_out, xn_rows_out = sem("x1_rows_out"), sem("xn_rows_out")
        slots_cleared, slots_written, slots_back = sem("slots_cleared"), sem("slots_written"), sem("slots_back")
        slots_turned = sem("slots_turned")
        slots_copied, rows_scaled, rows_cleared = sem("slots_copied"), sem("rows_scaled"), sem("rows_cleared")
        mask_in = [sem("mask_in0"), sem("mask_in1")]
        row_in = [sem("row_in0"), sem("row_in1")]
        weighted, idx_set = sem("weighted"), sem("idx_set")
        rows_turned, rows_copied, y_done, y_added = sem("rows_turned"), sem("rows_copied"), sem("y_done"), sem("y_added")
        y_out = [sem("y_out0"), sem("y_out1")]
        waited_dve, waited_pool = sem("waited_dve"), sem("waited_pool")

        out_rows = out.rearrange("b t n -> (b t) n")
        x_rows = x.rearrange("b (t p) n -> b p t n", p=P)
        wo_rows = wo.rearrange("(h d) n -> h d n", d=DH)
        rows_tiled = rows_d.rearrange("(t p) n -> p t n", p=P)

        block = ctx.enter_context(nc.Block())

        @block.sync
        def _(sp):
            sp.dma_start(acc[:, 0:NT, :], x_rows[0]).then_inc(x_in, 16)
            sp.dma_start(wq_in[:, :], wq[0]).then_inc(wq_landed, 16)
            sp.dma_start(wkv_in[:, :], wkv[0]).then_inc(wkv_landed, 16)
            for dst, src in ((ident, ident_in), (bo_t, bo), (cos_t, cosines), (sin_t, sines), (slopes, negslopes),
                             (near, reach_near), (far, reach_far)):
                sp.dma_start(dst[:, :], src).then_inc(consts_in, 16)
            sp.dma_start(slot_tokens_d.rearrange("(p t) o -> p (t o)", p=P), no_tokens_in[:, 0:SLOT_TILES]
                         ).then_inc(slots_cleared, 16)
            sp.wait_ge(x_in, 16)
            sp.dma_start(acc[:, NT:TILES, :], x_rows[1]).then_inc(x_in, 16)
            with sp.Fori(0, B) as b:
                with sp.Fori(0, G) as g:
                    it = b * G + g
                    for r in range(REP):
                        sp.wait_ge(wq_split_hi, it * REP + r + 1)
                        sp.wait_ge(wq_split_lo, it * REP + r + 1)
                        sp.dma_start(wq_in[:, :], wq[bass.ds(g * REP + (r + 1), 1)].rearrange("a p n -> (a p) n")
                                     ).then_inc(wq_landed, 16)
                        sp.wait_ge(wo_split_hi, it * REP + r + 1)
                        sp.wait_ge(wo_split_lo, it * REP + r + 1)
                        sp.dma_start(wo_in[:, :], wo_rows[bass.ds(g * REP + r, 1)].rearrange("a p n -> (a p) n")
                                     ).then_inc(wo_landed, 16)
                        if r == 0:
                            sp.wait_ge(wkv_split_hi, it + 1)
                            sp.wait_ge(wkv_split_lo, it + 1)
                            sp.dma_start(wkv_in[:, :], wkv[bass.ds(g + 1, 1)].rearrange("a p n -> (a p) n")
                                         ).then_inc(wkv_landed, 16)
            sp.wait_ge(out_added, 1 + B * G * OUTS_IT)
            for dst, src in ((router_t[:, :, :], router), (expert_ids[:, :, :], expert_ids_in),
                             (earlier[:, :], earlier_in), (token_ids[:, :], token_ids_in),
                             (tile_ids[:, :, :], tile_ids_in), (scale_t[:, :], scale),
                             (weight_t[:, :], weight), (slot_tok_i[:, SLOT_TILES:], past_end_in)):
                sp.dma_start(dst, src).then_inc(consts2_in, 16)
            sp.dma_start(rows_tiled[:, :, D:2 * D], acc[:, :, :]).then_inc(x1_rows_out, 16)
            sp.wait_ge(rows_scaled, TILES)
            sp.dma_start(rows_tiled[:, :, 0:D], xn[:, :, :]).then_inc(xn_rows_out, 16)
            sp.wait_ge(slots_written, 16 * TILES)
            sp.dma_start(slot_tok[:, :], slot_tokens_d.rearrange("(t p) o -> t (p o)", p=P)).then_inc(slots_back, 16)
            sp.wait_ge(route, EXPERTS_KNOWN)
            with sp.Fori(0, SLOT_TILES // 2) as n:
                for s in range(2):
                    sp.wait_ge(weighted, n * 2 + (s + 1))
                    e = sp.value_load(tile_expert_i[0:1, bass.ds(n * 2 + s, 1)], min_val=0, max_val=E - 1)
                    sp.dma_start(mask[:, s, :], masks[bass.ds(e, 1)].rearrange("a p n -> (a p) n")
                                 ).then_inc(mask_in[s], 16)

        @block.tensor
        def _(pe):
            mm = nc.tensor.matmul

            def product(dst, lhs, rhs, first=True, last=True, skip=False):
                (lh, ll), (rh, rl) = lhs, rhs
                mm(dst, lh, rh, start=first, stop=False, skip_group_check=skip)
                mm(dst, lh, rl, start=False, stop=False, skip_group_check=skip)
                return mm(dst, ll, rh, start=False, stop=last, skip_group_check=skip)

            for s in (pv_done, summed):
                pe.sem_inc(s, 1)
            pe.sem_inc(y_done, 2)
            pe.wait_ge(consts_in, 16 * CONSTS)
            pe.wait_ge(ones_set, 1)
            with pe.Fori(0, B) as b:
                for t in range(NT):
                    pe.wait_ge(ln_normed, b * NT + (t + 1))
                    if t < 2:
                        pe.wait_ge(out_added, b * (G * OUTS_IT) + 1)
                    else:
                        pe.wait_ge(ln_lo, b * NT + (t - 1))
                    for c in range(DC):
                        last = nc.tensor.transpose(work[:, t % 2, c * P:(c + 1) * P], xnorm[:, t % 2, c * P:(c + 1) * P],
                                                   ident[:, :])
                    last.then_inc(ln_turned, 1)
                with pe.Fori(0, G) as g:
                    it = b * G + g
                    job = [0]

                    def bank(kind, n):
                        j = job[0]
                        assert JOBS[j] == (kind, n), (JOBS[j], kind, n)
                        job[0] += 1
                        if j < 2:
                            pe.wait_ge(out_added, it * OUTS_IT + 1)
                            return work[:, j % 2, :]
                        was, m = JOBS[j - 2]
                        if was == "rope":
                            pe.wait_ge(rope_ready, it * ROPES_IT + (m + 1))
                        elif was == "vproj":
                            pe.wait_ge(v_copied, it * 2 + (m + 1))
                        elif was == "vturn":
                            pe.wait_ge(v_split_lo, it * 2 + (m + 1))
                        elif was == "sum":
                            pe.wait_ge(inverted, it * REP + (m + 1))
                        else:
                            pe.wait_ge(out_added, it * OUTS_IT + (m + 2))
                        return work[:, j % 2, :]

                    def project(kind, n, w, sig):
                        dst = bank(kind, n)
                        c0 = (n % 2) * 512
                        for c in range(DC):
                            last = product(dst, (w[0][:, c, :], w[1][:, c, :]),
                                           (xt_hi[:, c, c0:c0 + 512], xt_lo[:, c, c0:c0 + 512]), c == 0, c == DC - 1)
                        last.then_inc(sig, 1)

                    def project_q(r):
                        pe.wait_ge(wq_split_hi, it * REP + (r + 1))
                        pe.wait_ge(wq_split_lo, it * REP + (r + 1))
                        n = 2 * r + 2 if r else 0
                        for i in range(2):
                            project("rope", n + i, (wq_hi, wq_lo), projected)

                    def score(r, u):
                        c = r * NU + u
                        pe.wait_ge(rope_lo, it * ROPES_IT + (2 * r + 5))
                        pe.wait_ge(biased, it * UNITS_IT + (max(c - 1, 0) + 1))
                        for kt, qc, q0, w, col in UNITS[u]:
                            k = slice(kt * P, (kt + 1) * P)
                            q = slice(qc * 512 + q0, qc * 512 + q0 + w)
                            last = product(score_ps[:, c % 2, col:col + w], (k_hi[:, k], k_lo[:, k]),
                                           (q_hi[:, r % 2, q], q_lo[:, r % 2, q]))
                        last.then_inc(scored, 1)

                    def apply_v(r, u):
                        c = r * NU + u
                        s = c % P_SLOTS
                        pe.wait_ge(p_split_lo, it * UNITS_IT + (c + 1))
                        if u == 0:
                            pe.wait_ge(ctx_split_lo, (it * REP + r) * QC + 1)
                        if c == 0:
                            pe.wait_ge(v_split_lo, it * 2 + 2)
                        for kt, qc, q0, w, col in UNITS[u]:
                            last = product(ctx_ps[:, qc, q0:q0 + w], (v_hi[:, kt, :], v_lo[:, kt, :]),
                                           (p_hi[:, s, col:col + w], p_lo[:, s, col:col + w]),
                                           kt == (6 if qc else 0), kt == (7 if qc else 2), skip=True)
                        last.then_inc(pv_done, 1)

                    def sum_probs(r):
                        dst = bank("sum", r)
                        pe.wait_ge(p_added, (it * REP + r) * ADDS + (ADDS + 1))
                        for t in range(NT):
                            last = mm(dst[:, t:t + 1], psums[:, t * P:(t + 1) * P], ones[:, 0:1], start=True, stop=True)
                        last.then_inc(summed, 1)

                    def project_out(r, tiles):
                        pe.wait_ge(ctx_split_lo, (it * REP + r) * QC + (QC + 1))
                        pe.wait_ge(wo_split_hi, it * REP + (r + 2))
                        pe.wait_ge(wo_split_lo, it * REP + (r + 2))
                        for t in tiles:
                            dst = bank("out", r * NT + t)
                            q = slice(t * P, (t + 1) * P)
                            product(dst, (ctx_hi[:, q], ctx_lo[:, q]), (wo_hi[:, :], wo_lo[:, :])).then_inc(out_done, 1)

                    pe.wait_ge(ln_lo, b * NT + NT)
                    project_q(0)
                    pe.wait_ge(wkv_split_hi, it + 1)
                    pe.wait_ge(wkv_split_lo, it + 1)
                    for n in range(2):
                        project("rope", 2 + n, (wkv_hi[:, 0], wkv_lo[:, 0]), projected)
                    for n in range(2):
                        project("vproj", n, (wkv_hi[:, 1], wkv_lo[:, 1]), v_projected)
                    for n in range(2):
                        dst = bank("vturn", n)
                        pe.wait_ge(v_copied, it * 2 + (n + 1))
                        for i in range(4):
                            k = n * 4 + i
                            last = nc.tensor.transpose(dst[:, i * P:(i + 1) * P], v_rows[:, k * P:(k + 1) * P], ident[:, :])
                        last.then_inc(v_turned, 1)
                    for r in range(REP):
                        score(r, 0)
                        score(r, 1)
                        if r:
                            sum_probs(r - 1)
                            project_out(r - 1, (0, 1))
                        score(r, 2)
                        if r:
                            project_out(r - 1, (2, 3))
                        apply_v(r, 0)
                        if r:
                            project_out(r - 1, (4, 5))
                        score(r, 3)
                        apply_v(r, 1)
                        if r:
                            project_out(r - 1, (6, 7))
                        score(r, 4)
                        if r < REP - 1:
                            project_q(r + 1)
                        apply_v(r, 2)
                        apply_v(r, 3)
                        apply_v(r, 4)
                    sum_probs(REP - 1)
                    project_out(REP - 1, range(NT))
                    assert job[0] == len(JOBS)

            pe.wait_ge(consts2_in, 16 * CONSTS2)
            for t in range(TILES):
                pe.wait_ge(l2_normed, t + 1)
                if t:
                    pe.wait_ge(l2_copied, t)
                for c in range(DC):
                    last = nc.tensor.transpose(work[:, 0, c * P:(c + 1) * P], xn[:, t, c * P:(c + 1) * P], ident[:, :])
                last.then_inc(l2_turned, 1)
                pe.wait_ge(l2_copied, t + 1)
                if t:
                    pe.wait_ge(l2_kept, t)
                for c in range(DC):
                    last = mm(work[:, 1, 0:E], xn_t[:, t % 2, c * P:(c + 1) * P], router_t[:, c, :],
                              start=c == 0, stop=c == DC - 1)
                last.then_inc(l2_logits, 1)
            pe.wait_ge(route, HOT_KNOWN)
            hot = one_hot[:, :, :].rearrange("p t e -> p (t e)")
            mm(score_ps[:, 0, 0:512], earlier[:, :], hot, start=True, stop=True).then_inc(ranked, 1)
            mm(score_ps[:, 1, 0:512], ones[:, :], hot, start=True, stop=True).then_inc(ranked, 1)
            pe.wait_ge(slots_back, 16)
            nc.tensor.transpose(ctx_ps[:, 0, 0:SLOT_TILES], slot_tok[:, :], ident[0:SLOT_TILES, 0:SLOT_TILES]
                                ).then_inc(slots_turned, 1)

            def turn_rows(m, s):
                for c in range(DC):
                    last = nc.tensor.transpose(ctx_ps[:, s, c * P:(c + 1) * P], row[s][:, c * P:(c + 1) * P], ident[:, :])
                last.then_inc(rows_turned, 1)

            pe.wait_ge(slots_copied, 1)
            pe.wait_ge(row_in[0], 16)
            turn_rows(0, 0)
            with pe.Fori(0, SLOT_TILES // 2) as n:
                for s in range(2):
                    if s == 0:
                        pe.wait_ge(row_in[1], n * 16 + 16)
                    else:
                        pe.wait_ge(row_in[0], n * 16 + 32)
                    pe.wait_ge(rows_copied, n * 2 + (s + 1))
                    turn_rows(s + 1, 1 - s)
                    pe.wait_ge(rows_copied, n * 2 + (s + 2))
                    pe.wait_ge(weighted, n * 2 + (s + 3))
                    pe.wait_ge(y_added, n * 2 + (s + 1))
                    for c in range(DC):
                        last = mm(work[:, s, :], row_t[:, s, c * P:(c + 1) * P], w_exp[:, s, c, :],
                                  start=c == 0, stop=c == DC - 1)
                    last.then_inc(y_done, 1)

        @block.scalar
        def _(act):
            f = nc.scalar.activation
            for s in (wo_split_hi, rows_copied):
                act.sem_inc(s, 1)

            def split_wq():
                f(wq_hi[:, :, :].rearrange("p c n -> p (c n)"), wq_in[:, :], ACT.Copy).then_inc(wq_split_hi, 1)

            def split_wkv():
                f(wkv_hi[:, :, :, :].rearrange("p a c n -> p (a c n)"), wkv_in[:, :], ACT.Copy).then_inc(wkv_split_hi, 1)

            act.wait_ge(wq_landed, 16)
            split_wq()
            act.wait_ge(wkv_landed, 16)
            split_wkv()
            with act.Fori(0, B) as b:
                act.wait_ge(ln_step, b * LN_STEPS + (2 * NT + 1))
                f(rs[:, 1, 0:NT], rs[:, 0, 0:NT], ACT.Sqrt).then_inc(ln_root, 1)
                for t in range(NT):
                    act.wait_ge(ln_turned, b * NT + (t + 1))
                    f(xt_hi[:, :, t * P:(t + 1) * P], work[:, t % 2, :].rearrange("p (c n) -> p c n", c=DC),
                      ACT.Copy).then_inc(ln_hi, 1)
                with act.Fori(0, G) as g:
                    it = b * G + g

                    def rope_part(n, dst):
                        act.wait_ge(rope_sum, it * ROPES_IT + (n + 1))
                        f(dst, rope_a[:, n % 2, :], ACT.Copy).then_inc(rope_hi, 1)

                    def tanh_exp(r, u):
                        c = r * NU + u
                        s, w = c % P_SLOTS, WIDTH[u]
                        act.wait_ge(biased, it * UNITS_IT + (c + 2))
                        f(probs[:, s, 0:w], probs[:, s, 0:w], ACT.Tanh, scale=1.0 / (TANH_CAP * DH ** 0.5)
                          ).then_inc(tanhed, 1)
                        act.wait_ge(tanhed, it * UNITS_IT + (c + 1))
                        f(probs[:, s, 0:w], probs[:, s, 0:w], ACT.Exp, scale=TANH_CAP).then_inc(exped, 1)

                    def split(r, u):
                        c = r * NU + u
                        s, w = c % P_SLOTS, WIDTH[u]
                        act.wait_ge(exped, it * UNITS_IT + (c + 1))
                        if MASK_RANK[u]:
                            act.wait_ge(masked, (it * REP + r) * MASKS + MASK_RANK[u])
                        f(p_hi[:, s, 0:w], probs[:, s, 0:w], ACT.Copy).then_inc(p_split_hi, 1)

                    def split_ctx(r, qc):
                        act.wait_ge(pv_done, (it * REP + r) * NU + ((3, 6)[qc]))
                        f(ctx_hi[:, qc * 512:(qc + 1) * 512], ctx_ps[:, qc, :], ACT.Copy).then_inc(ctx_split_hi, 1)

                    for n in range(4):
                        a = (n % 2) * 512
                        rope_part(n, q_hi[:, 0, a:a + 512] if n < 2 else k_hi[:, a:a + 512])
                    for n in range(2):
                        act.wait_ge(v_projected, it * 2 + (n + 1))
                        f(v_rows[:, n * 512:(n + 1) * 512], work[:, n, :], ACT.Copy).then_inc(v_copied, 1)
                    for n in range(2):
                        act.wait_ge(v_turned, it * 2 + (n + 1))
                        f(v_hi[:, n * 4:(n + 1) * 4, :].rearrange("p k d -> p (k d)"), work[:, n, :],
                          ACT.Copy).then_inc(v_split_hi, 1)
                    for r in range(REP):
                        n = 4 + 2 * r
                        tanh_exp(r, 0)
                        act.wait_ge(wq_landed, (it * REP + r) * 16 + 32)
                        split_wq()
                        tanh_exp(r, 1)
                        split(r, 0)
                        tanh_exp(r, 2)
                        split(r, 1)
                        if r == 1:
                            act.wait_ge(wkv_landed, it * 16 + 32)
                            split_wkv()
                        tanh_exp(r, 3)
                        split(r, 2)
                        tanh_exp(r, 4)
                        split(r, 3)
                        if r < REP - 1:
                            rope_part(n, q_hi[:, (r + 1) % 2, 0:512])
                        split(r, 4)
                        if r < REP - 1:
                            rope_part(n + 1, q_hi[:, (r + 1) % 2, 512:1024])
                        act.wait_ge(wo_landed, (it * REP + r) * 16 + 16)
                        f(wo_hi[:, :], wo_in[:, :], ACT.Copy).then_inc(wo_split_hi, 1)
                        split_ctx(r, 0)
                        split_ctx(r, 1)

            act.wait_ge(l2_step, 2 * TILES + 1)
            f(rs[:, 1, :], rs[:, 0, :], ACT.Sqrt).then_inc(l2_root, 1)
            for t in range(TILES):
                act.wait_ge(l2_turned, t + 1)
                f(xn_t[:, t % 2, :], work[:, 0, :], ACT.Copy).then_inc(l2_copied, 1)
            act.wait_ge(route, SHIFTED)
            f(expo[:, :, :], expo[:, :, :], ACT.Exp).then_inc(route_exp, 1)
            act.wait_ge(rows_turned, 1)
            f(row_t[:, 0, :], ctx_ps[:, 0, :], ACT.Copy).then_inc(rows_copied, 1)
            with act.Fori(0, SLOT_TILES // 2) as n:
                for s in range(2):
                    act.wait_ge(rows_turned, n * 2 + (s + 2))
                    act.wait_ge(y_done, n * 2 + (s + 2))
                    f(row_t[:, 1 - s, :], ctx_ps[:, 1 - s, :], ACT.Copy).then_inc(rows_copied, 1)

        @block.vector
        def _(dve):
            v = nc.vector
            for s in (biased, ctx_split_lo, out_added):
                dve.sem_inc(s, 1)
            for s in (weighted, y_added):
                dve.sem_inc(s, 2)
            v.memset(ones[:, :], 1.0).then_inc(ones_set, 1)

            def norm_stats(tile, tiles, step, root, base, done):
                k = 0
                for t in range(tiles):
                    v.bn_stats(stats[:, t, :], tile(t)).then_inc(step, 1)
                k += tiles
                dve.wait_ge(step, base + k)
                dve.sem_inc(waited_dve, 1)
                for t in range(tiles):
                    v.bn_aggr(mean_var[:, t, :], stats[:, t, :]).then_inc(step, 1)
                k += tiles
                dve.wait_ge(step, base + k)
                a, root_a, y0, z = (rs[:, i, 0:tiles] for i in range(4))
                v.tensor_scalar(a, mean_var[:, 0:tiles, 1], LN_EPS, None, ALU.add).then_inc(step, 1)
                dve.wait_ge(root, done)
                v.reciprocal(y0, root_a).then_inc(step, 1)
                dve.wait_ge(step, base + (k + 2))
                v.tensor_tensor(z, y0, y0, ALU.mult).then_inc(step, 1)
                dve.wait_ge(step, base + (k + 3))
                v.scalar_tensor_tensor(out=z, in0=z, scalar=-0.5, in1=a, op0=ALU.mult, op1=ALU.mult).then_inc(step, 1)
                dve.wait_ge(step, base + (k + 4))
                v.scalar_tensor_tensor(out=y0, in0=z, scalar=1.5, in1=y0, op0=ALU.add, op1=ALU.mult).then_inc(step, 1)
                dve.wait_ge(step, base + (k + 5))

            dve.wait_ge(consts_in, 16 * CONSTS)
            with dve.Fori(0, B) as b:
                def x_tile(t):
                    return acc[:, bass.ds(b * NT + t, 1), :].rearrange("p a n -> p (a n)")

                dve.wait_ge(x_in, b * 16 + 16)
                norm_stats(x_tile, NT, ln_step, ln_root, b * LN_STEPS, b + 1)

                def split_turned(t):
                    dve.wait_ge(ln_hi, b * NT + (t + 1))
                    v.tensor_tensor(xt_lo[:, :, t * P:(t + 1) * P], work[:, t % 2, :].rearrange("p (c n) -> p c n", c=DC),
                                    xt_hi[:, :, t * P:(t + 1) * P].bitcast(F32), ALU.subtract).then_inc(ln_lo, 1)

                for t in range(NT):
                    if t > 1:
                        split_turned(t - 2)
                    v.tensor_scalar(xnorm[:, t % 2, :], x_tile(t), mean_var[:, t, 0:1], rs[:, 2, t:t + 1],
                                    ALU.subtract, ALU.mult).then_inc(ln_normed, 1)
                split_turned(NT - 2)
                split_turned(NT - 1)
                with dve.Fori(0, G) as g:
                    it = b * G + g

                    def rotate(n):
                        pos = slice((n % 2) * 512, (n % 2) * 512 + 512)
                        src, i = work[:, JOBS.index(("rope", n)) % 2, :], n % 2
                        dve.wait_ge(projected, it * ROPES_IT + (n + 1))
                        dve.wait_ge(rope_lo, it * ROPES_IT + (max(n - 1, 0) + 1))
                        v.tensor_tensor(rope_a[:, i, :], src, cos_t[:, pos], ALU.mult)
                        v.tensor_tensor(rope_b[0:64, i, :], src[64:128, :], sin_t[64:128, pos], ALU.mult)
                        v.tensor_tensor(rope_b[64:128, i, :], src[0:64, :], sin_t[0:64, pos], ALU.mult
                                        ).then_inc(rope_ready, 1)

                    def bias(r, u):
                        c = r * NU + u
                        s, w = c % P_SLOTS, WIDTH[u]
                        dve.wait_ge(scored, it * UNITS_IT + (c + 1))
                        if c < P_SLOTS:
                            dve.wait_ge(pv_done, it * UNITS_IT + 1)
                            dve.wait_ge(p_added, it * (REP * ADDS) + 1)
                        else:
                            rr, uu = divmod(c - P_SLOTS, NU)
                            dve.wait_ge(pv_done, it * UNITS_IT + (rr * NU + uu + 2))
                            dve.wait_ge(p_added, it * (REP * ADDS) + (rr * ADDS + ADD_RANK[uu] + 1))
                        slope = slopes[:, bass.ds(g * REP + r, 1)]
                        if u in (2, 3):
                            a = 256 if u == 2 else 0
                            pairs = [(probs[:, s, 0:512], far[:, a:a + 512], score_ps[:, c % 2, 0:512]),
                                     (probs[:, s, 512:1024], far[:, a + 128:a + 640], score_ps[:, c % 2, 512:1024])]
                        elif u == 1:
                            halves = [near[:, :], probs[:, s, 0:512], score_ps[:, c % 2, 0:512]]
                            n_, p_, s_ = (z.rearrange("p (a c) -> p a c", a=2) for z in halves)
                            pairs = [(p_, n_[:, :, 0:256], s_)]
                        else:
                            pairs = [(probs[:, s, :], near[:, :], score_ps[:, c % 2, :])]
                        for dst, reach, src in pairs:
                            last = v.scalar_tensor_tensor(out=dst, in0=reach, scalar=slope, in1=src,
                                                          op0=ALU.mult, op1=ALU.add)
                        last.then_inc(biased, 1)

                    def split(r, u):
                        c = r * NU + u
                        s, w = c % P_SLOTS, WIDTH[u]
                        dve.wait_ge(p_split_hi, it * UNITS_IT + (c + 1))
                        v.tensor_tensor(p_lo[:, s, 0:w], probs[:, s, 0:w], p_hi[:, s, 0:w].bitcast(F32), ALU.subtract
                                        ).then_inc(p_split_lo, 1)

                    def split_ctx(r, qc):
                        dve.wait_ge(ctx_split_hi, (it * REP + r) * QC + (qc + 1))
                        q = slice(qc * 512, (qc + 1) * 512)
                        v.tensor_tensor(ctx_lo[:, q], ctx_ps[:, qc, :], ctx_hi[:, q].bitcast(F32), ALU.subtract
                                        ).then_inc(ctx_split_lo, 1)

                    def invert(r):
                        dve.wait_ge(summed, it * REP + (r + 2))
                        v.reciprocal(rinv[:, :], work[:, JOBS.index(("sum", r)) % 2, 0:NT]).then_inc(inverted, 1)

                    def add_out(r, tiles):
                        if 0 in tiles:
                            dve.wait_ge(inverted, it * REP + (r + 1))
                        for t in tiles:
                            n = r * NT + t
                            dve.wait_ge(out_done, it * OUTS_IT + (n + 1))
                            dve.wait_ge(out_added, it * OUTS_IT + (max(n - NT + 1, 0) + 1))
                            v.scalar_tensor_tensor(out=x_tile(t), in0=work[:, JOBS.index(("out", n)) % 2, :],
                                                   scalar=rinv[:, t:t + 1], in1=x_tile(t), op0=ALU.mult, op1=ALU.add
                                                   ).then_inc(out_added, 1)

                    for n in range(4):
                        rotate(n)
                    for n in range(2):
                        dve.wait_ge(v_split_hi, it * 2 + (n + 1))
                        v.tensor_tensor(v_lo[:, n * 4:(n + 1) * 4, :].rearrange("p k d -> p (k d)"), work[:, n, :],
                                        v_hi[:, n * 4:(n + 1) * 4, :].rearrange("p k d -> p (k d)").bitcast(F32),
                                        ALU.subtract).then_inc(v_split_lo, 1)
                    dve.wait_ge(bias_added, b * NT + NT)
                    for r in range(REP):
                        bias(r, 0)
                        bias(r, 1)
                        if r:
                            invert(r - 1)
                            add_out(r - 1, (0, 1))
                        bias(r, 2)
                        if r:
                            add_out(r - 1, (2, 3))
                        split(r, 0)
                        if r:
                            add_out(r - 1, (4, 5))
                        split(r, 1)
                        bias(r, 3)
                        if r:
                            add_out(r - 1, (6, 7))
                        split(r, 2)
                        bias(r, 4)
                        if r < REP - 1:
                            rotate(4 + 2 * r)
                            rotate(5 + 2 * r)
                        split(r, 3)
                        split(r, 4)
                        split_ctx(r, 0)
                        split_ctx(r, 1)
                    invert(REP - 1)
                    add_out(REP - 1, range(NT))

            dve.wait_ge(out_added, 1 + B * G * OUTS_IT)
            norm_stats(lambda t: acc[:, t, :], TILES, l2_step, l2_root, 0, 1)
            for t in range(TILES):
                v.tensor_scalar(xn[:, t, :], acc[:, t, :], mean_var[:, t, 0:1], rs[:, 2, t:t + 1],
                                ALU.subtract, ALU.mult).then_inc(l2_normed, 1)
                if t:
                    dve.wait_ge(l2_logits, t)
                    v.tensor_copy(logits[:, t - 1, :], work[:, 1, 0:E]).then_inc(l2_kept, 1)
            dve.wait_ge(l2_logits, TILES)
            v.tensor_copy(logits[:, TILES - 1, :], work[:, 1, 0:E]).then_inc(l2_kept, 1)
            dve.wait_ge(l2_kept, TILES)
            dve.wait_ge(consts2_in, 16 * CONSTS2)

            count = [0]

            def step(ins):
                count[0] += 1
                ins.then_inc(route, 1)
                dve.wait_ge(route, count[0])

            def over_experts(ap):
                return ap.rearrange("p (t a) -> p t a", a=1).to_broadcast([P, TILES, E])

            step(v.tensor_reduce(top[:, :], logits[:, :, :], AX.X, ALU.max))
            step(v.tensor_tensor(expo[:, :, :], logits[:, :, :], over_experts(top[:, :]), ALU.subtract))
            assert count[0] == SHIFTED
            step(v.tensor_tensor(one_hot[:, :, :], logits[:, :, :], over_experts(top[:, :]), ALU.is_equal))
            step(v.scalar_tensor_tensor(out=rank[:, :, :], in0=one_hot[:, :, :], scalar=float(-E),
                                        in1=expert_ids[:, :, :], op0=ALU.mult, op1=ALU.add))
            step(v.tensor_reduce(first[:, :], rank[:, :, :], AX.X, ALU.min))
            step(v.tensor_scalar(first[:, :], first[:, :], float(E), None, ALU.add))
            step(v.tensor_tensor(one_hot[:, :, :], expert_ids[:, :, :], over_experts(first[:, :]), ALU.is_equal))
            assert count[0] == HOT_KNOWN
            dve.wait_ge(route_exp, 1)
            step(v.tensor_reduce(top_w[:, 0, :], expo[:, :, :], AX.X, ALU.add))
            step(v.reciprocal(top_w[:, 1, :], top_w[:, 0, :]))
            step(v.memset(before[:, 0, :], 0.0))
            dve.wait_ge(ranked, 2)
            for t in range(TILES):
                step(v.tensor_tensor(before[:, t + 1, :], score_ps[:, 1, t * E:(t + 1) * E], before[:, t, :], ALU.add))
            step(v.tensor_scalar(expert_tiles_i[:, 0, :], before[:, TILES, :], float(P - 1), None, ALU.add))
            step(v.tensor_scalar(expert_tiles_i[:, 1, :], expert_tiles_i[:, 0, :], 7, None, ALU.logical_shift_right))
            step(v.tensor_copy(expert_tiles[:, 0, :], expert_tiles_i[:, 1, :]))
            step(v.tensor_tensor_scan(expert_tiles[:, 1, :], ones[:, 0:E], expert_tiles[:, 0, :], 0.0, ALU.mult, ALU.add))
            step(v.tensor_tensor(expert_tiles[:, 2, :], expert_tiles[:, 1, :], expert_tiles[:, 0, :], ALU.subtract))
            step(v.tensor_tensor(rank[:, :, :].rearrange("p t e -> p (t e)"), score_ps[:, 0, 0:512],
                                 before[:, 0:TILES, :].rearrange("p t e -> p (t e)"), ALU.add))
            step(v.scalar_tensor_tensor(out=rank[:, :, :], in0=expert_tiles[:, 2:3, :].to_broadcast([P, TILES, E]),
                                        scalar=float(P), in1=rank[:, :, :], op0=ALU.mult, op1=ALU.add))
            step(v.tensor_tensor(rank[:, :, :], rank[:, :, :], one_hot[:, :, :], ALU.mult))
            step(v.tensor_reduce(slot_f[:, :], rank[:, :, :], AX.X, ALU.add))
            step(v.tensor_copy(slot_i[:, :], slot_f[:, :]))
            assert count[0] == SLOTS_KNOWN
            step(v.tensor_tensor(tile_past[:, :, :], tile_ids[:, :, :],
                                 expert_tiles[0:1, 1:2, :].to_broadcast([1, SLOT_TILES, E]), ALU.is_ge))
            step(v.tensor_reduce(tile_expert[:, :], tile_past[:, :, :], AX.X, ALU.add))
            step(v.tensor_scalar(tile_expert_i[:, :], tile_expert[:, :], float(E - 1), None, ALU.min))
            assert count[0] == EXPERTS_KNOWN
            for t in range(TILES):
                v.tensor_scalar(xn[:, t, :], xn[:, t, :], top_w[:, 1, t:t + 1], None, ALU.mult).then_inc(rows_scaled, 1)
            step(v.tensor_scalar(weight_t[:, :], weight_t[:, :], 2.0, 1.0, ALU.mult, ALU.min))
            step(v.tensor_scalar(weight_t[:, :], weight_t[:, :], -1.0, ROUND, ALU.max, ALU.add))
            step(v.tensor_scalar(weight_t[:, :], weight_t[:, :], ROUND, None, ALU.subtract))
            w3 = weight_t[:, :].rearrange("p (c n) -> p c n", c=DC)
            step(v.tensor_tensor(w3, w3, scale_t[:, :].rearrange("p (a n) -> p a n", a=1).to_broadcast([P, DC, D]), ALU.mult))
            dve.wait_ge(slots_turned, 1)
            v.tensor_copy(slot_tok_i[:, 0:SLOT_TILES], ctx_ps[:, 0, 0:SLOT_TILES]).then_inc(slots_copied, 1)
            with dve.Fori(0, SLOT_TILES // 2) as n:
                for s in range(2):
                    dve.wait_ge(mask_in[s], n * 16 + 16)
                    dve.wait_ge(y_done, n * 2 + (s + 1))
                    v.tensor_tensor(w_exp[:, s, :, :].rearrange("p c n -> p (c n)"), mask[:, s, :], weight_t[:, :],
                                    ALU.mult).then_inc(weighted, 1)
                for s in range(2):
                    dve.wait_ge(y_done, n * 2 + (s + 3))
                    dve.wait_ge(y_out[s], n * 16 + 16)
                    v.tensor_tensor(y[s][:, :], work[:, s, :], row[s][:, D:2 * D], ALU.add).then_inc(y_added, 1)

        @block.gpsimd
        def _(pool):
            p = nc.gpsimd
            for s in (rope_lo, p_added, wo_split_lo):
                pool.sem_inc(s, 1)

            def split_wq():
                p.tensor_tensor(wq_lo[:, :, :].rearrange("p c n -> p (c n)"), wq_in[:, :],
                                wq_hi[:, :, :].rearrange("p c n -> p (c n)").bitcast(F32), ALU.subtract
                                ).then_inc(wq_split_lo, 1)

            def split_wkv():
                p.tensor_tensor(wkv_lo[:, :, :, :].rearrange("p a c n -> p (a c n)"), wkv_in[:, :],
                                wkv_hi[:, :, :, :].rearrange("p a c n -> p (a c n)").bitcast(F32), ALU.subtract
                                ).then_inc(wkv_split_lo, 1)

            pool.wait_ge(wq_split_hi, 1)
            split_wq()
            pool.wait_ge(wkv_split_hi, 1)
            split_wkv()
            pool.wait_ge(consts_in, 16 * CONSTS)
            with pool.Fori(0, B) as b:
                for t in range(NT):
                    pool.wait_ge(ln_normed, b * NT + (t + 1))
                    tile = acc[:, bass.ds(b * NT + t, 1), :].rearrange("p a n -> p (a n)")
                    p.tensor_tensor(tile, tile, bo_t[:, :], ALU.add).then_inc(bias_added, 1)
                with pool.Fori(0, G) as g:
                    it = b * G + g

                    def rope_add(n):
                        pool.wait_ge(rope_ready, it * ROPES_IT + (n + 1))
                        i = n % 2
                        p.tensor_tensor(rope_a[:, i, :], rope_a[:, i, :], rope_b[:, i, :], ALU.add).then_inc(rope_sum, 1)

                    def rope_split(n, dst, hi):
                        pool.wait_ge(rope_hi, it * ROPES_IT + (n + 1))
                        p.tensor_tensor(dst, rope_a[:, n % 2, :], hi.bitcast(F32), ALU.subtract).then_inc(rope_lo, 1)

                    def past_only(r, u):
                        c = r * NU + u
                        s = c % P_SLOTS
                        pool.wait_ge(exped, it * UNITS_IT + (c + 1))
                        pool.sem_inc(waited_pool, 1)
                        two = probs[:, s, 0:512 if u == 1 else 1024].rearrange("p (a c) -> p a c", a=2)[:, :, 0:P]
                        last = p.affine_select(out=two, in_=two, compare_op=ALU.is_ge, fill=0.0, base=0,
                                               pattern=[[0, 2], [1, P]], channel_multiplier=-1)
                        if u != 1:
                            one = probs[:, s, 896:1024]
                            last = p.affine_select(out=one, in_=one, compare_op=ALU.is_ge, fill=0.0, base=0,
                                                   pattern=[[1, P]], channel_multiplier=-1)
                        last.then_inc(masked, 1)
                        pool.wait_ge(masked, (it * REP + r) * MASKS + MASK_RANK[u])

                    def add_probs(r, k, q0, q1, a, b_=None):
                        done = (it * REP + r) * ADDS + k
                        pool.wait_ge(p_added, done)
                        if b_ is None:
                            p.tensor_tensor(psums[:, q0:q1], psums[:, q0:q1], a, ALU.add).then_inc(p_added, 1)
                        else:
                            p.tensor_tensor(psums[:, q0:q1], a, b_, ALU.add).then_inc(p_added, 1)

                    for n in range(4):
                        rope_add(n)
                        a = (n % 2) * 512
                        hi, lo = (q_hi[:, 0, a:a + 512], q_lo[:, 0, a:a + 512]) if n < 2 else \
                            (k_hi[:, a:a + 512], k_lo[:, a:a + 512])
                        rope_split(n, lo, hi)
                    for r in range(REP):
                        def pr(u, c0, c1):
                            return probs[:, (r * NU + u) % P_SLOTS, c0:c1]

                        past_only(r, 0)
                        pool.wait_ge(summed, it * REP + (r + 1))
                        add_probs(r, 1, P, 512, pr(0, P, 512), pr(0, 512, 896))
                        pool.wait_ge(p_added, (it * REP + r) * ADDS + 2)
                        p.tensor_tensor(psums[:, 0:P], pr(0, 0, P), ones[:, :], ALU.mult).then_inc(p_added, 1)
                        add_probs(r, 3, 384, 512, pr(0, 896, 1024))
                        past_only(r, 1)
                        add_probs(r, 4, 256, 512, pr(1, 0, 256))
                        pool.wait_ge(wq_split_hi, it * REP + (r + 2))
                        split_wq()
                        pool.wait_ge(exped, it * UNITS_IT + (r * NU + 3))
                        add_probs(r, 5, 512, 1024, pr(2, 0, 512), pr(2, 512, 1024))
                        add_probs(r, 6, 768, 1024, pr(1, 256, 512))
                        if r == 1:
                            pool.wait_ge(wkv_split_hi, it + 2)
                            split_wkv()
                        pool.wait_ge(exped, it * UNITS_IT + (r * NU + 4))
                        add_probs(r, 7, 512, 1024, pr(3, 0, 512))
                        add_probs(r, 8, 512, 1024, pr(3, 512, 1024))
                        n = 4 + 2 * r
                        if r < REP - 1:
                            rope_add(n)
                        past_only(r, 4)
                        if r < REP - 1:
                            rope_split(n, q_lo[:, (r + 1) % 2, 0:512], q_hi[:, (r + 1) % 2, 0:512])
                            rope_add(n + 1)
                            rope_split(n + 1, q_lo[:, (r + 1) % 2, 512:1024], q_hi[:, (r + 1) % 2, 512:1024])
                        add_probs(r, 9, 512, 1024, pr(4, 0, 512))
                        add_probs(r, 10, 640, 1024, pr(4, 512, 896))
                        add_probs(r, 11, 896, 1024, pr(4, 896, 1024))
                        pool.wait_ge(wo_split_hi, it * REP + (r + 2))
                        p.tensor_tensor(wo_lo[:, :], wo_in[:, :], wo_hi[:, :].bitcast(F32), ALU.subtract
                                        ).then_inc(wo_split_lo, 1)

            def store(s):
                p.indirect_dma_start(out_rows, bass.IndirectOffsetOnAxis(ap=out_idx[s][:, :], axis=0), y[s][:, :],
                                     None, bounds_check=B * T - 1, oob_is_err=False).then_inc(y_out[s], 16)

            pool.wait_ge(out_added, 1 + B * G * OUTS_IT)
            for s in range(2):
                p.memset(row[s][:, :], 0.0).then_inc(rows_cleared, 1)
                p.memset(y[s][:, :], 0.0).then_inc(rows_cleared, 1)
                p.memset(out_idx[s][:, :], NO_TOKEN).then_inc(rows_cleared, 1)
            pool.wait_ge(rows_cleared, 6)
            for s in range(2):
                store(s)
            pool.wait_ge(consts2_in, 16 * CONSTS2)
            pool.wait_ge(slots_cleared, 16)
            pool.wait_ge(route, SLOTS_KNOWN)
            for t in range(TILES):
                p.indirect_dma_start(slot_tokens_d, bass.IndirectOffsetOnAxis(ap=slot_i[:, t:t + 1], axis=0),
                                     token_ids[:, t:t + 1], None).then_inc(slots_written, 16)

            def fetch(i, s, gathered):
                if gathered is not None:
                    pool.wait_ge(row_in[s], gathered)
                    pool.sem_inc(waited_pool, 1)
                p.tensor_copy(row_idx[s][:, :], slot_tok_i[:, i]).then_inc(idx_set, 1)

            def gather(s):
                p.indirect_dma_start(row[s][:, :], None, rows_d, bass.IndirectOffsetOnAxis(ap=row_idx[s][:, :], axis=0),
                                     bounds_check=B * T - 1, oob_is_err=False).then_inc(row_in[s], 16)

            pool.wait_ge(slots_copied, 1)
            pool.wait_ge(x1_rows_out, 16)
            pool.wait_ge(xn_rows_out, 16)
            for s in range(2):
                fetch(slice(s, s + 1), s, None)
                pool.wait_ge(idx_set, s + 1)
                gather(s)
            with pool.Fori(0, SLOT_TILES // 2) as n:
                for s in range(2):
                    pool.wait_ge(y_out[s], n * 16 + 16)
                    pool.sem_inc(waited_pool, 1)
                    p.tensor_copy(out_idx[s][:, :], slot_tok_i[:, bass.ds(n * 2 + s, 1)]).then_inc(idx_set, 1)
                    fetch(bass.ds(n * 2 + (s + 2), 1), s, n * 16 + 16)
                    pool.wait_ge(idx_set, n * 4 + (2 * s + 4))
                    pool.wait_ge(y_added, n * 2 + (s + 3))
                    pool.sem_inc(waited_pool, 1)
                    store(s)
                    gather(s)
            for s in range(2):
                pool.wait_ge(y_out[s], 16 * (SLOT_TILES // 2) + 16)
                pool.wait_ge(row_in[s], 16 * (SLOT_TILES // 2) + 16)


def tables():
    inv_freq = (np.float32(1.0) / np.float32(ROPE_THETA) ** (np.arange(0, DH, 2, dtype=np.float32) / np.float32(DH)))
    angle = (np.arange(T, dtype=np.float32)[:, None] * inv_freq[None, :].astype(np.float32)).T
    cosines = np.concatenate([np.cos(angle)] * 2).astype(np.float32)
    sines = np.concatenate([np.sin(angle), -np.sin(angle)]).astype(np.float32)
    key = np.arange(P, dtype=np.float32)[:, None]
    near = np.concatenate([np.arange(w) for w in (512, 384, 128)]).astype(np.float32)[None, :] - key
    far = np.arange(P, 1024, dtype=np.float32)[None, :] - key
    slopes = 2.0 ** (-np.arange(1, H + 1, dtype=np.float32) * np.float32(8.0 / H))
    spread = np.ones((P, 1), np.float32)
    experts = np.arange(E, dtype=np.float32)
    return {
        "cosines": cosines, "sines": sines, "negslopes": -spread * slopes[None, :].astype(np.float32),
        "reach_near": near, "reach_far": far, "ident_in": np.eye(P, dtype=np.float32),
        "earlier_in": np.triu(np.ones((P, P), np.float32), 1),
        "expert_ids_in": np.tile(experts, (P, TILES, 1)),
        "tile_ids_in": np.repeat(np.arange(SLOT_TILES, dtype=np.float32), E).reshape(1, SLOT_TILES, E),
        "token_ids_in": (np.arange(TILES) * P + np.arange(P)[:, None]).astype(np.float32),
        "no_tokens_in": np.full((P, SLOT_TILES), NO_TOKEN, np.float32),
        "past_end_in": np.full((P, 2), NO_TOKEN, np.uint32),
    }


def kernel(**inputs):
    from concourse import bacc
    from concourse.bass_utils import run_bass_kernel_spmd

    a = {k.split("_", 2)[2]: np.ascontiguousarray(v) for k, v in inputs.items()}
    halves = np.concatenate([np.arange(0, DH, 2), np.arange(1, DH, 2)])

    def by_head(w, order=slice(None)):
        return w.reshape(DC, P, -1, DH)[..., order].transpose(2, 1, 0, 3).reshape(-1, P, DC * DH)

    wq = by_head(a["Wq"], halves)
    wkv = np.stack([by_head(a["Wk"], halves), by_head(a["Wv"])], axis=2).reshape(G, P, 2 * DC * DH)
    arrays = {
        "x": a["hidden_states"],
        "wq": np.concatenate([wq, wq[:1]]),
        "wkv": np.concatenate([wkv, wkv[:1]]),
        "wo": a["Wo"],
        "bo": np.tile(a["bo"], (P, 1)),
        "router": a["router_w"].T.reshape(DC, P, E).transpose(1, 0, 2),
        "weight": a["weight"].T.reshape(DC, P, D).transpose(1, 0, 2).reshape(P, DC * D),
        "scale": np.tile(a["scale"], (P, 1)),
        "masks": a["expert_masks"].transpose(0, 2, 1).reshape(E, DC, P, D).transpose(0, 2, 1, 3).reshape(E, P, DC * D),
        **tables(),
    }
    arrays = {f"{k}_dram": np.ascontiguousarray(v) for k, v in arrays.items()}
    nc = bacc.Bacc("TRN2", target_bir_lowering=False, num_devices=1)
    args = {k[:-5]: nc.dram_tensor(k, v.shape, mybir.dt.from_np(v.dtype), kind="ExternalInput").ap()
            for k, v in arrays.items()}
    args["rows_d"] = nc.dram_tensor("rows_scratch", (B * T, 2 * D), F32, kind="Internal").ap()
    args["slot_tokens_d"] = nc.dram_tensor("slot_tokens_scratch", (SLOT_TILES * P, 1), F32, kind="Internal").ap()
    args["out"] = nc.dram_tensor("out_dram", (B, T, D), F32, kind="ExternalOutput").ap()
    block_kernel(nc, **args)
    r = run_bass_kernel_spmd(nc, [arrays], core_ids=[0])
    return r.results[0]["out_dram"]
```

```python
from contextlib import ExitStack

import numpy as np

import concourse.bass as bass
from concourse import mybir

ALU = mybir.AluOpType
ACT = mybir.ActivationFunctionType
AX = mybir.AxisListType
F32 = mybir.dt.float32
F32R = mybir.dt.float32r
I32 = mybir.dt.int32
U32 = mybir.dt.uint32

P = 128
B, T, D = 2, 1024, 512
H, G, DH = 16, 4, 128
REP = H // G
E = 32
NT = T // P
TILES = B * NT
DC = D // P
QC = T // 512
LN_EPS = 1e-5
ROPE_THETA = 10000.0
TANH_CAP = 30.0
OVERFLOW_TILES = TILES
SLOT_TILES = E + OVERFLOW_TILES
STEP, ROWS = 8, 4
NO_TOKEN = 2 * B * T
ROUND = 1.5 * 2.0 ** 23

UNITS = [
    [(0, 0, 0, 512, 0), (1, 0, 128, 384, 512), (3, 0, 384, 128, 896)],
    [(2, 0, 256, 256, 0), (6, 1, 256, 256, 256)],
    [(1, 1, 0, 512, 0), (0, 1, 0, 512, 512)],
    [(3, 1, 0, 512, 0), (2, 1, 0, 512, 512)],
    [(4, 1, 0, 512, 0), (5, 1, 128, 384, 512), (7, 1, 384, 128, 896)],
]
NU = len(UNITS)
WIDTH = [sum(e[3] for e in u) for u in UNITS]
DIAGONAL = [True, True, False, False, True]
ADDS = 11
ADD_RANK = [3, 6, 5, 8, 11]
MASKS = 3
MASK_RANK = [1, 2, None, None, 3]
UNITS_IT = REP * NU
P_SLOTS = 3
ROPES_IT = 2 * REP + 2
OUTS_IT = REP * NT
LN_STEPS = 2 * NT + 5
CONSTS = 7
CONSTS2 = 7
SHIFTED, HOT_KNOWN, SLOTS_KNOWN, EXPERTS_KNOWN = 2, 7, 42, 46


def bank_jobs():
    jobs = [("rope", n) for n in range(4)] + [("vproj", 0), ("vproj", 1), ("vturn", 0), ("vturn", 1)]
    rope = 4
    for r in range(REP):
        if r:
            jobs += [("sum", r - 1)] + [("out", (r - 1) * NT + t) for t in range(NT)]
        if r < REP - 1:
            jobs += [("rope", rope), ("rope", rope + 1)]
            rope += 2
    jobs += [("sum", REP - 1)] + [("out", (REP - 1) * NT + t) for t in range(NT)]
    return jobs


JOBS = bank_jobs()
assert len(JOBS) % 2 == 0


def block_kernel(nc, x, wq, wkv, wo, bo, cosines, sines, negslopes, reach_near, reach_far, ident_in, earlier_in,
                 expert_ids_in, tile_ids_in, token_ids_in, no_tokens_in, router, weight, scale,
                 masks, rows_d, slot_tokens_d, out):
    ctx = ExitStack()
    with ctx:
        attn = ExitStack()

        def sb(name, shape, dt=F32, stack=ctx):
            return stack.enter_context(nc.sbuf_tensor(name, shape, dt))

        def asb(name, shape, dt=F32):
            return sb(name, shape, dt, attn)

        def sem(name):
            return ctx.enter_context(nc.semaphore(name))

        acc = sb("acc", [P, TILES, D])
        ident = sb("ident", [P, P])
        ones = sb("ones", [P, P])
        mean_var = sb("mean_var", [P, TILES, 2])
        stats = sb("stats", [P, TILES, 6])
        rs = sb("rs", [P, 4, TILES])
        xnorm = sb("xnorm", [P, 2, D])

        xt_hi = asb("xt_hi", [P, DC, T], F32R)
        xt_lo = asb("xt_lo", [P, DC, T], F32R)
        k_hi = asb("k_hi", [P, T], F32R)
        k_lo = asb("k_lo", [P, T], F32R)
        v_rows = asb("v_rows", [P, T])
        v_hi = asb("v_hi", [P, NT, DH], F32R)
        v_lo = asb("v_lo", [P, NT, DH], F32R)
        q_hi = asb("q_hi", [P, 2, T], F32R)
        q_lo = asb("q_lo", [P, 2, T], F32R)
        probs = asb("probs", [P, P_SLOTS, 1024])
        p_hi = asb("p_hi", [P, P_SLOTS, 1024], F32R)
        p_lo = asb("p_lo", [P, P_SLOTS, 1024], F32R)
        psums = asb("psums", [P, T])
        ctx_hi = asb("ctx_hi", [P, T], F32R)
        ctx_lo = asb("ctx_lo", [P, T], F32R)
        rinv = asb("rinv", [P, NT])
        wq_in = asb("wq_in", [P, DC * DH])
        wq_hi = asb("wq_hi", [P, DC, DH], F32R)
        wq_lo = asb("wq_lo", [P, DC, DH], F32R)
        wo_in = asb("wo_in", [P, D])
        wo_hi = asb("wo_hi", [P, D], F32R)
        wo_lo = asb("wo_lo", [P, D], F32R)
        wkv_in = asb("wkv_in", [P, 2 * DC * DH])
        wkv_hi = asb("wkv_hi", [P, 2, DC, DH], F32R)
        wkv_lo = asb("wkv_lo", [P, 2, DC, DH], F32R)
        cos_t = asb("cos_t", [P, T])
        sin_t = asb("sin_t", [P, T])
        rope_a = asb("rope_a", [P, 2, 512])
        rope_b = asb("rope_b", [P, 2, 512])
        bo_t = asb("bo_t", [P, D])
        slopes = asb("slopes", [P, H])
        far = asb("far", [P, 7 * P])
        near = asb("near", [P, 1024])
        attn.close()

        xn = sb("xn", [P, TILES, D])
        xn_t = sb("xn_t", [P, 4, D])
        router_t = sb("router_t", [P, DC, E])
        logits = sb("logits", [P, TILES, E])
        expo = sb("expo", [P, TILES, E])
        top = sb("top", [P, TILES])
        first = sb("first", [P, TILES])
        top_w = sb("top_w", [P, 2, TILES])
        expert_ids = sb("expert_ids", [P, TILES, E])
        one_hot = sb("one_hot", [P, TILES, E])
        rank = sb("rank", [P, TILES, E])
        before = sb("before", [P, TILES + 1, E])
        earlier = sb("earlier", [P, P])
        more_tiles = sb("more_tiles", [P, 3, E])
        more_tiles_i = sb("more_tiles_i", [P, 2, E], I32)
        slot_parts = sb("slot_parts", [P, 3, TILES])
        slot_f = sb("slot_f", [P, TILES])
        slot_i = sb("slot_i", [P, TILES], U32)
        token_ids = sb("token_ids", [P, TILES])
        tile_ids = sb("tile_ids", [1, OVERFLOW_TILES, E])
        tile_past = sb("tile_past", [1, OVERFLOW_TILES, E])
        tile_expert = sb("tile_expert", [1, OVERFLOW_TILES])
        tile_expert_i = sb("tile_expert_i", [1, OVERFLOW_TILES], I32)
        overflow_i = sb("overflow_i", [1, 1], I32)
        slot_tok = sb("slot_tok", [SLOT_TILES, P])
        slot_tok_i = sb("slot_tok_i", [P, SLOT_TILES], U32)
        weight_t = sb("weight_t", [P, DC * D])
        scale_t = sb("scale_t", [P, D])
        mask = sb("mask", [P, STEP, DC * D])
        row = [sb(f"row{i}", [P, 2 * D]) for i in range(ROWS)]
        row_t = sb("row_t", [P, 2, D])
        row_idx = [sb(f"row_idx{i}", [P, 1], U32) for i in range(ROWS)]
        out_idx = [sb(f"out_idx{i}", [P, 1], U32) for i in range(ROWS)]
        y = [sb(f"y{i}", [P, D]) for i in range(ROWS)]

        score_ps = ctx.enter_context(nc.psum_tensor("score_ps", [P, 2, 1024], F32))
        ctx_ps = ctx.enter_context(nc.psum_tensor("ctx_ps", [P, 2, 512], F32))
        work = ctx.enter_context(nc.psum_tensor("work", [P, 2, 512], F32))

        consts_in = sem("consts_in")
        x_in = sem("x_in")
        wq_landed, wo_landed, wkv_landed = sem("wq_landed"), sem("wo_landed"), sem("wkv_landed")
        wq_split_hi, wq_split_lo = sem("wq_split_hi"), sem("wq_split_lo")
        wo_split_hi, wo_split_lo = sem("wo_split_hi"), sem("wo_split_lo")
        wkv_split_hi, wkv_split_lo = sem("wkv_split_hi"), sem("wkv_split_lo")
        ones_set = sem("ones_set")
        ln_step, ln_root, ln_normed = sem("ln_step"), sem("ln_root"), sem("ln_normed")
        ln_turned, ln_hi, ln_lo = sem("ln_turned"), sem("ln_hi"), sem("ln_lo")
        bias_added = sem("bias_added")
        projected = sem("projected")
        rope_ready, rope_sum, rope_hi, rope_lo = sem("rope_ready"), sem("rope_sum"), sem("rope_hi"), sem("rope_lo")
        v_projected, v_copied = sem("v_projected"), sem("v_copied")
        v_turned, v_split_hi, v_split_lo = sem("v_turned"), sem("v_split_hi"), sem("v_split_lo")
        scored, biased, tanhed, exped, masked = (sem("scored"), sem("biased"), sem("tanhed"), sem("exped"),
                                                 sem("masked"))
        p_split_hi, p_split_lo, p_added = sem("p_split_hi"), sem("p_split_lo"), sem("p_added")
        pv_done = sem("pv_done")
        ctx_split_hi, ctx_split_lo = sem("ctx_split_hi"), sem("ctx_split_lo")
        summed, inverted = sem("summed"), sem("inverted")
        out_done, out_added = sem("out_done"), sem("out_added")
        consts2_in = sem("consts2_in")
        l2_step, l2_root, l2_normed = sem("l2_step"), sem("l2_root"), sem("l2_normed")
        l2_turned, l2_copied = sem("l2_turned"), sem("l2_copied")
        l2_logits, l2_kept = sem("l2_logits"), sem("l2_kept")
        route, route_exp, ranked = sem("route"), sem("route_exp"), sem("ranked")
        x1_rows_out, xn_rows_out = sem("x1_rows_out"), sem("xn_rows_out")
        slots_cleared, slots_written, slots_back = sem("slots_cleared"), sem("slots_written"), sem("slots_back")
        slots_turned = sem("slots_turned")
        slots_copied, rows_scaled, rows_cleared = sem("slots_copied"), sem("rows_scaled"), sem("rows_cleared")
        mask_in = [sem(f"mask_in{i}") for i in range(STEP)]
        row_in = [sem(f"row_in{i}") for i in range(ROWS)]
        weighted, idx_set = sem("weighted"), sem("idx_set")
        rows_turned, rows_copied, y_done, y_added = sem("rows_turned"), sem("rows_copied"), sem("y_done"), sem("y_added")
        y_out = [sem(f"y_out{i}") for i in range(ROWS)]
        waited_dve, waited_pool = sem("waited_dve"), sem("waited_pool")

        out_rows = out.rearrange("b t n -> (b t) n")
        x_rows = x.rearrange("b (t p) n -> b p t n", p=P)
        wo_rows = wo.rearrange("(h d) n -> h d n", d=DH)
        rows_tiled = rows_d.rearrange("(t p) n -> p t n", p=P)

        block = ctx.enter_context(nc.Block())

        @block.sync
        def _(sp):
            sp.dma_start(acc[:, 0:NT, :], x_rows[0]).then_inc(x_in, 16)
            sp.dma_start(wq_in[:, :], wq[0]).then_inc(wq_landed, 16)
            sp.dma_start(wkv_in[:, :], wkv[0]).then_inc(wkv_landed, 16)
            for dst, src in ((ident, ident_in), (bo_t, bo), (cos_t, cosines), (sin_t, sines), (slopes, negslopes),
                             (near, reach_near), (far, reach_far)):
                sp.dma_start(dst[:, :], src).then_inc(consts_in, 16)
            sp.dma_start(slot_tokens_d.rearrange("(p t) o -> p (t o)", p=P), no_tokens_in[:, 0:SLOT_TILES]
                         ).then_inc(slots_cleared, 16)
            sp.wait_ge(x_in, 16)
            sp.dma_start(acc[:, NT:TILES, :], x_rows[1]).then_inc(x_in, 16)
            with sp.Fori(0, B) as b:
                with sp.Fori(0, G) as g:
                    it = b * G + g
                    for r in range(REP):
                        sp.wait_ge(wq_split_hi, it * REP + r + 1)
                        sp.wait_ge(wq_split_lo, it * REP + r + 1)
                        sp.dma_start(wq_in[:, :], wq[bass.ds(g * REP + (r + 1), 1)].rearrange("a p n -> (a p) n")
                                     ).then_inc(wq_landed, 16)
                        sp.wait_ge(wo_split_hi, it * REP + r + 1)
                        sp.wait_ge(wo_split_lo, it * REP + r + 1)
                        sp.dma_start(wo_in[:, :], wo_rows[bass.ds(g * REP + r, 1)].rearrange("a p n -> (a p) n")
                                     ).then_inc(wo_landed, 16)
                        if r == 0:
                            sp.wait_ge(wkv_split_hi, it + 1)
                            sp.wait_ge(wkv_split_lo, it + 1)
                            sp.dma_start(wkv_in[:, :], wkv[bass.ds(g + 1, 1)].rearrange("a p n -> (a p) n")
                                         ).then_inc(wkv_landed, 16)
            sp.wait_ge(out_added, 1 + B * G * OUTS_IT)
            for dst, src in ((router_t[:, :, :], router), (expert_ids[:, :, :], expert_ids_in),
                             (earlier[:, :], earlier_in), (token_ids[:, :], token_ids_in),
                             (tile_ids[:, :, :], tile_ids_in), (scale_t[:, :], scale),
                             (weight_t[:, :], weight)):
                sp.dma_start(dst, src).then_inc(consts2_in, 16)
            sp.dma_start(rows_tiled[:, :, D:2 * D], acc[:, :, :]).then_inc(x1_rows_out, 16)
            for s in range(STEP):
                sp.dma_start(mask[:, s, :], masks[s]).then_inc(mask_in[s], 16)
            sp.wait_ge(rows_scaled, TILES)
            sp.dma_start(rows_tiled[:, :, 0:D], xn[:, :, :]).then_inc(xn_rows_out, 16)
            sp.wait_ge(slots_written, 16 * TILES)
            sp.dma_start(slot_tok[:, :], slot_tokens_d.rearrange("(t p) o -> t (p o)", p=P)).then_inc(slots_back, 16)
            with sp.Fori(0, E // STEP - 1) as n:
                for s in range(STEP):
                    sp.wait_ge(y_done, n * STEP + (s + 3))
                    sp.dma_start(mask[:, s, :], masks[bass.ds(n * STEP + (s + STEP), 1)].rearrange("a p n -> (a p) n")
                                 ).then_inc(mask_in[s], 16)
            sp.wait_ge(route, EXPERTS_KNOWN)
            with sp.If(sp.value_load(overflow_i[0:1, 0:1], min_val=0, max_val=OVERFLOW_TILES) > 0):
                with sp.Fori(0, OVERFLOW_TILES // STEP) as n:
                    for s in range(STEP):
                        sp.wait_ge(y_done, n * STEP + (E - STEP + s + 3))
                        e = sp.value_load(tile_expert_i[0:1, bass.ds(n * STEP + s, 1)], min_val=0, max_val=E - 1)
                        sp.dma_start(mask[:, s, :], masks[bass.ds(e, 1)].rearrange("a p n -> (a p) n")
                                     ).then_inc(mask_in[s], 16)

        @block.tensor
        def _(pe):
            mm = nc.tensor.matmul

            def product(dst, lhs, rhs, first=True, last=True, skip=False):
                (lh, ll), (rh, rl) = lhs, rhs
                mm(dst, lh, rh, start=first, stop=False, skip_group_check=skip)
                mm(dst, lh, rl, start=False, stop=False, skip_group_check=skip)
                return mm(dst, ll, rh, start=False, stop=last, skip_group_check=skip)

            for s in (pv_done, summed):
                pe.sem_inc(s, 1)
            pe.sem_inc(y_done, 2)
            pe.wait_ge(consts_in, 16 * CONSTS)
            pe.wait_ge(ones_set, 1)
            with pe.Fori(0, B) as b:
                for t in range(NT):
                    pe.wait_ge(ln_normed, b * NT + (t + 1))
                    if t < 2:
                        pe.wait_ge(out_added, b * (G * OUTS_IT) + 1)
                    else:
                        pe.wait_ge(ln_lo, b * NT + (t - 1))
                    for c in range(DC):
                        last = nc.tensor.transpose(work[:, t % 2, c * P:(c + 1) * P], xnorm[:, t % 2, c * P:(c + 1) * P],
                                                   ident[:, :])
                    last.then_inc(ln_turned, 1)
                with pe.Fori(0, G) as g:
                    it = b * G + g
                    job = [0]

                    def bank(kind, n):
                        j = job[0]
                        assert JOBS[j] == (kind, n), (JOBS[j], kind, n)
                        job[0] += 1
                        if j < 2:
                            pe.wait_ge(out_added, it * OUTS_IT + 1)
                            return work[:, j % 2, :]
                        was, m = JOBS[j - 2]
                        if was == "rope":
                            pe.wait_ge(rope_ready, it * ROPES_IT + (m + 1))
                        elif was == "vproj":
                            pe.wait_ge(v_copied, it * 2 + (m + 1))
                        elif was == "vturn":
                            pe.wait_ge(v_split_lo, it * 2 + (m + 1))
                        elif was == "sum":
                            pe.wait_ge(inverted, it * REP + (m + 1))
                        else:
                            pe.wait_ge(out_added, it * OUTS_IT + (m + 2))
                        return work[:, j % 2, :]

                    def project(kind, n, w, sig):
                        dst = bank(kind, n)
                        c0 = (n % 2) * 512
                        for c in range(DC):
                            last = product(dst, (w[0][:, c, :], w[1][:, c, :]),
                                           (xt_hi[:, c, c0:c0 + 512], xt_lo[:, c, c0:c0 + 512]), c == 0, c == DC - 1)
                        last.then_inc(sig, 1)

                    def project_q(r):
                        pe.wait_ge(wq_split_hi, it * REP + (r + 1))
                        pe.wait_ge(wq_split_lo, it * REP + (r + 1))
                        n = 2 * r + 2 if r else 0
                        for i in range(2):
                            project("rope", n + i, (wq_hi, wq_lo), projected)

                    def score(r, u):
                        c = r * NU + u
                        pe.wait_ge(rope_lo, it * ROPES_IT + (2 * r + 5))
                        pe.wait_ge(biased, it * UNITS_IT + (max(c - 1, 0) + 1))
                        for kt, qc, q0, w, col in UNITS[u]:
                            k = slice(kt * P, (kt + 1) * P)
                            q = slice(qc * 512 + q0, qc * 512 + q0 + w)
                            last = product(score_ps[:, c % 2, col:col + w], (k_hi[:, k], k_lo[:, k]),
                                           (q_hi[:, r % 2, q], q_lo[:, r % 2, q]))
                        last.then_inc(scored, 1)

                    def apply_v(r, u):
                        c = r * NU + u
                        s = c % P_SLOTS
                        pe.wait_ge(p_split_lo, it * UNITS_IT + (c + 1))
                        if u == 0:
                            pe.wait_ge(ctx_split_lo, (it * REP + r) * QC + 1)
                        if c == 0:
                            pe.wait_ge(v_split_lo, it * 2 + 2)
                        for kt, qc, q0, w, col in UNITS[u]:
                            last = product(ctx_ps[:, qc, q0:q0 + w], (v_hi[:, kt, :], v_lo[:, kt, :]),
                                           (p_hi[:, s, col:col + w], p_lo[:, s, col:col + w]),
                                           kt == (6 if qc else 0), kt == (7 if qc else 2), skip=True)
                        last.then_inc(pv_done, 1)

                    def sum_probs(r):
                        dst = bank("sum", r)
                        pe.wait_ge(p_added, (it * REP + r) * ADDS + (ADDS + 1))
                        for t in range(NT):
                            last = mm(dst[:, t:t + 1], psums[:, t * P:(t + 1) * P], ones[:, 0:1], start=True, stop=True)
                        last.then_inc(summed, 1)

                    def project_out(r, tiles):
                        pe.wait_ge(ctx_split_lo, (it * REP + r) * QC + (QC + 1))
                        pe.wait_ge(wo_split_hi, it * REP + (r + 2))
                        pe.wait_ge(wo_split_lo, it * REP + (r + 2))
                        for t in tiles:
                            dst = bank("out", r * NT + t)
                            q = slice(t * P, (t + 1) * P)
                            product(dst, (ctx_hi[:, q], ctx_lo[:, q]), (wo_hi[:, :], wo_lo[:, :])).then_inc(out_done, 1)

                    pe.wait_ge(ln_lo, b * NT + NT)
                    project_q(0)
                    pe.wait_ge(wkv_split_hi, it + 1)
                    pe.wait_ge(wkv_split_lo, it + 1)
                    for n in range(2):
                        project("rope", 2 + n, (wkv_hi[:, 0], wkv_lo[:, 0]), projected)
                    for n in range(2):
                        project("vproj", n, (wkv_hi[:, 1], wkv_lo[:, 1]), v_projected)
                    for n in range(2):
                        dst = bank("vturn", n)
                        pe.wait_ge(v_copied, it * 2 + (n + 1))
                        for i in range(4):
                            k = n * 4 + i
                            last = nc.tensor.transpose(dst[:, i * P:(i + 1) * P], v_rows[:, k * P:(k + 1) * P], ident[:, :])
                        last.then_inc(v_turned, 1)
                    for r in range(REP):
                        score(r, 0)
                        score(r, 1)
                        if r:
                            sum_probs(r - 1)
                            project_out(r - 1, (0, 1))
                        score(r, 2)
                        if r:
                            project_out(r - 1, (2, 3))
                        apply_v(r, 0)
                        if r:
                            project_out(r - 1, (4, 5))
                        score(r, 3)
                        apply_v(r, 1)
                        if r:
                            project_out(r - 1, (6, 7))
                        score(r, 4)
                        if r < REP - 1:
                            project_q(r + 1)
                        apply_v(r, 2)
                        apply_v(r, 3)
                        apply_v(r, 4)
                    sum_probs(REP - 1)
                    project_out(REP - 1, range(NT))
                    assert job[0] == len(JOBS)

            pe.wait_ge(consts2_in, 16 * CONSTS2)
            pe.wait_ge(out_added, 1 + B * G * OUTS_IT)

            def turn_xn(t):
                pe.wait_ge(l2_normed, t + 1)
                if t > 3:
                    pe.wait_ge(l2_copied, t - 3)
                for c in range(DC):
                    last = nc.tensor.transpose(score_ps[:, t % 4 // 2, t % 2 * D + c * P:t % 2 * D + (c + 1) * P],
                                               xn[:, t, c * P:(c + 1) * P], ident[:, :])
                last.then_inc(l2_turned, 1)

            turn_xn(0)
            for t in range(TILES):
                if t < TILES - 1:
                    turn_xn(t + 1)
                pe.wait_ge(l2_copied, t + 1)
                for c in range(DC):
                    last = mm(work[:, 1, t * E:(t + 1) * E], xn_t[:, t % 4, c * P:(c + 1) * P], router_t[:, c, :],
                              start=c == 0, stop=c == DC - 1)
                last.then_inc(l2_logits, 1)
            pe.wait_ge(route, HOT_KNOWN)
            hot = one_hot[:, :, :].rearrange("p t e -> p (t e)")
            mm(score_ps[:, 0, 0:512], earlier[:, :], hot, start=True, stop=True).then_inc(ranked, 1)
            mm(score_ps[:, 1, 0:512], ones[:, :], hot, start=True, stop=True).then_inc(ranked, 1)
            pe.wait_ge(slots_back, 16)
            nc.tensor.transpose(ctx_ps[:, 0, 0:SLOT_TILES], slot_tok[:, :], ident[0:SLOT_TILES, 0:SLOT_TILES]
                                ).then_inc(slots_turned, 1)

            def turn_rows(n, s):
                pe.wait_ge(row_in[s % ROWS], n * (16 * STEP // ROWS) + 16 * (s // ROWS + 1))
                for c in range(DC):
                    last = nc.tensor.transpose(ctx_ps[:, s % 2, c * P:(c + 1) * P],
                                               row[s % ROWS][:, c * P:(c + 1) * P], ident[:, :])
                last.then_inc(rows_turned, 1)

            def multiply(n, s):
                pe.wait_ge(rows_copied, n * STEP + (s + 2))
                pe.wait_ge(weighted, n * STEP + (s + 1))
                pe.wait_ge(y_added, n * STEP + (s + 1))
                for c in range(DC):
                    last = mm(work[:, s % 2, :], row_t[:, s % 2, c * P:(c + 1) * P], mask[:, s, c * D:(c + 1) * D],
                              start=c == 0, stop=c == DC - 1)
                last.then_inc(y_done, 1)

            def expert_tiles(n, last):
                for s in range(STEP):
                    if s < STEP - 1 or not last:
                        pe.wait_ge(rows_copied, n * STEP + (s + 1))
                        turn_rows(n if s < STEP - 1 else n + 1, (s + 1) % STEP)
                    multiply(n, s)

            pe.wait_ge(slots_copied, 1)
            turn_rows(0, 0)
            with pe.Fori(0, E // STEP - 1) as n:
                expert_tiles(n, False)
            expert_tiles(E // STEP - 1, True)
            pe.wait_ge(route, EXPERTS_KNOWN)
            with pe.If(pe.value_load(overflow_i[0:1, 0:1], min_val=0, max_val=OVERFLOW_TILES) > 0):
                with pe.Fori(0, OVERFLOW_TILES // STEP) as n:
                    for s in range(STEP):
                        pe.wait_ge(rows_copied, n * STEP + (E + s))
                        turn_rows(n + E // STEP, s)
                        multiply(n + E // STEP, s)

        @block.scalar
        def _(act):
            f = nc.scalar.activation
            for s in (wo_split_hi, rows_copied):
                act.sem_inc(s, 1)

            def split_wq():
                f(wq_hi[:, :, :].rearrange("p c n -> p (c n)"), wq_in[:, :], ACT.Copy).then_inc(wq_split_hi, 1)

            def split_wkv():
                f(wkv_hi[:, :, :, :].rearrange("p a c n -> p (a c n)"), wkv_in[:, :], ACT.Copy).then_inc(wkv_split_hi, 1)

            act.wait_ge(wq_landed, 16)
            split_wq()
            act.wait_ge(wkv_landed, 16)
            split_wkv()
            with act.Fori(0, B) as b:
                act.wait_ge(ln_step, b * LN_STEPS + (2 * NT + 1))
                f(rs[:, 1, 0:NT], rs[:, 0, 0:NT], ACT.Sqrt).then_inc(ln_root, 1)
                for t in range(NT):
                    act.wait_ge(ln_turned, b * NT + (t + 1))
                    f(xt_hi[:, :, t * P:(t + 1) * P], work[:, t % 2, :].rearrange("p (c n) -> p c n", c=DC),
                      ACT.Copy).then_inc(ln_hi, 1)
                with act.Fori(0, G) as g:
                    it = b * G + g

                    def rope_part(n, dst):
                        act.wait_ge(rope_sum, it * ROPES_IT + (n + 1))
                        f(dst, rope_a[:, n % 2, :], ACT.Copy).then_inc(rope_hi, 1)

                    def tanh_exp(r, u):
                        c = r * NU + u
                        s, w = c % P_SLOTS, WIDTH[u]
                        act.wait_ge(biased, it * UNITS_IT + (c + 2))
                        f(probs[:, s, 0:w], probs[:, s, 0:w], ACT.Tanh, scale=1.0 / (TANH_CAP * DH ** 0.5)
                          ).then_inc(tanhed, 1)
                        act.wait_ge(tanhed, it * UNITS_IT + (c + 1))
                        f(probs[:, s, 0:w], probs[:, s, 0:w], ACT.Exp, scale=TANH_CAP).then_inc(exped, 1)

                    def split(r, u):
                        c = r * NU + u
                        s, w = c % P_SLOTS, WIDTH[u]
                        act.wait_ge(exped, it * UNITS_IT + (c + 1))
                        if MASK_RANK[u]:
                            act.wait_ge(masked, (it * REP + r) * MASKS + MASK_RANK[u])
                        f(p_hi[:, s, 0:w], probs[:, s, 0:w], ACT.Copy).then_inc(p_split_hi, 1)

                    def split_ctx(r, qc):
                        act.wait_ge(pv_done, (it * REP + r) * NU + ((3, 6)[qc]))
                        f(ctx_hi[:, qc * 512:(qc + 1) * 512], ctx_ps[:, qc, :], ACT.Copy).then_inc(ctx_split_hi, 1)

                    for n in range(4):
                        a = (n % 2) * 512
                        rope_part(n, q_hi[:, 0, a:a + 512] if n < 2 else k_hi[:, a:a + 512])
                    for n in range(2):
                        act.wait_ge(v_projected, it * 2 + (n + 1))
                        f(v_rows[:, n * 512:(n + 1) * 512], work[:, n, :], ACT.Copy).then_inc(v_copied, 1)
                    for n in range(2):
                        act.wait_ge(v_turned, it * 2 + (n + 1))
                        f(v_hi[:, n * 4:(n + 1) * 4, :].rearrange("p k d -> p (k d)"), work[:, n, :],
                          ACT.Copy).then_inc(v_split_hi, 1)
                    for r in range(REP):
                        n = 4 + 2 * r
                        tanh_exp(r, 0)
                        act.wait_ge(wq_landed, (it * REP + r) * 16 + 32)
                        split_wq()
                        tanh_exp(r, 1)
                        split(r, 0)
                        tanh_exp(r, 2)
                        split(r, 1)
                        if r == 1:
                            act.wait_ge(wkv_landed, it * 16 + 32)
                            split_wkv()
                        tanh_exp(r, 3)
                        split(r, 2)
                        tanh_exp(r, 4)
                        split(r, 3)
                        if r < REP - 1:
                            rope_part(n, q_hi[:, (r + 1) % 2, 0:512])
                        split(r, 4)
                        if r < REP - 1:
                            rope_part(n + 1, q_hi[:, (r + 1) % 2, 512:1024])
                        act.wait_ge(wo_landed, (it * REP + r) * 16 + 16)
                        f(wo_hi[:, :], wo_in[:, :], ACT.Copy).then_inc(wo_split_hi, 1)
                        split_ctx(r, 0)
                        split_ctx(r, 1)

            act.wait_ge(l2_step, 2 * TILES + 1)
            f(rs[:, 1, :], rs[:, 0, :], ACT.Sqrt).then_inc(l2_root, 1)
            for t in range(TILES):
                act.wait_ge(l2_turned, t + 1)
                if t > 3:
                    act.wait_ge(l2_logits, t - 3)
                f(xn_t[:, t % 4, :], score_ps[:, t % 4 // 2, t % 2 * D:(t % 2 + 1) * D], ACT.Copy).then_inc(l2_copied, 1)
            act.wait_ge(route, SHIFTED)
            f(expo[:, :, :], expo[:, :, :], ACT.Exp).then_inc(route_exp, 1)
            def keep_rows(n, s):
                act.wait_ge(rows_turned, n * STEP + (s + 1))
                act.wait_ge(y_done, n * STEP + (s + 1))
                f(row_t[:, s % 2, :], ctx_ps[:, s % 2, :], ACT.Copy).then_inc(rows_copied, 1)

            with act.Fori(0, E // STEP) as n:
                for s in range(STEP):
                    keep_rows(n, s)
            act.wait_ge(route, EXPERTS_KNOWN)
            with act.If(act.value_load(overflow_i[0:1, 0:1], min_val=0, max_val=OVERFLOW_TILES) > 0):
                with act.Fori(0, OVERFLOW_TILES // STEP) as n:
                    for s in range(STEP):
                        keep_rows(n + E // STEP, s)

        @block.vector
        def _(dve):
            v = nc.vector
            for s in (biased, ctx_split_lo, out_added):
                dve.sem_inc(s, 1)
            dve.sem_inc(y_added, 2)
            v.memset(ones[:, :], 1.0).then_inc(ones_set, 1)

            def norm_stats(tile, tiles, step, root, base, done):
                k = 0
                for t in range(tiles):
                    v.bn_stats(stats[:, t, :], tile(t)).then_inc(step, 1)
                k += tiles
                dve.wait_ge(step, base + k)
                dve.sem_inc(waited_dve, 1)
                for t in range(tiles):
                    v.bn_aggr(mean_var[:, t, :], stats[:, t, :]).then_inc(step, 1)
                k += tiles
                dve.wait_ge(step, base + k)
                a, root_a, y0, z = (rs[:, i, 0:tiles] for i in range(4))
                v.tensor_scalar(a, mean_var[:, 0:tiles, 1], LN_EPS, None, ALU.add).then_inc(step, 1)
                dve.wait_ge(root, done)
                v.reciprocal(y0, root_a).then_inc(step, 1)
                dve.wait_ge(step, base + (k + 2))
                v.tensor_tensor(z, y0, y0, ALU.mult).then_inc(step, 1)
                dve.wait_ge(step, base + (k + 3))
                v.scalar_tensor_tensor(out=z, in0=z, scalar=-0.5, in1=a, op0=ALU.mult, op1=ALU.mult).then_inc(step, 1)
                dve.wait_ge(step, base + (k + 4))
                v.scalar_tensor_tensor(out=y0, in0=z, scalar=1.5, in1=y0, op0=ALU.add, op1=ALU.mult).then_inc(step, 1)
                dve.wait_ge(step, base + (k + 5))

            dve.wait_ge(consts_in, 16 * CONSTS)
            with dve.Fori(0, B) as b:
                def x_tile(t):
                    return acc[:, bass.ds(b * NT + t, 1), :].rearrange("p a n -> p (a n)")

                dve.wait_ge(x_in, b * 16 + 16)
                norm_stats(x_tile, NT, ln_step, ln_root, b * LN_STEPS, b + 1)

                def split_turned(t):
                    dve.wait_ge(ln_hi, b * NT + (t + 1))
                    v.tensor_tensor(xt_lo[:, :, t * P:(t + 1) * P], work[:, t % 2, :].rearrange("p (c n) -> p c n", c=DC),
                                    xt_hi[:, :, t * P:(t + 1) * P].bitcast(F32), ALU.subtract).then_inc(ln_lo, 1)

                for t in range(NT):
                    if t > 1:
                        split_turned(t - 2)
                    v.tensor_scalar(xnorm[:, t % 2, :], x_tile(t), mean_var[:, t, 0:1], rs[:, 2, t:t + 1],
                                    ALU.subtract, ALU.mult).then_inc(ln_normed, 1)
                split_turned(NT - 2)
                split_turned(NT - 1)
                with dve.Fori(0, G) as g:
                    it = b * G + g

                    def rotate(n):
                        pos = slice((n % 2) * 512, (n % 2) * 512 + 512)
                        src, i = work[:, JOBS.index(("rope", n)) % 2, :], n % 2
                        dve.wait_ge(projected, it * ROPES_IT + (n + 1))
                        dve.wait_ge(rope_lo, it * ROPES_IT + (max(n - 1, 0) + 1))
                        v.tensor_tensor(rope_a[:, i, :], src, cos_t[:, pos], ALU.mult)
                        v.tensor_tensor(rope_b[0:64, i, :], src[64:128, :], sin_t[64:128, pos], ALU.mult)
                        v.tensor_tensor(rope_b[64:128, i, :], src[0:64, :], sin_t[0:64, pos], ALU.mult
                                        ).then_inc(rope_ready, 1)

                    def bias(r, u):
                        c = r * NU + u
                        s, w = c % P_SLOTS, WIDTH[u]
                        dve.wait_ge(scored, it * UNITS_IT + (c + 1))
                        if c < P_SLOTS:
                            dve.wait_ge(pv_done, it * UNITS_IT + 1)
                            dve.wait_ge(p_added, it * (REP * ADDS) + 1)
                        else:
                            rr, uu = divmod(c - P_SLOTS, NU)
                            dve.wait_ge(pv_done, it * UNITS_IT + (rr * NU + uu + 2))
                            dve.wait_ge(p_added, it * (REP * ADDS) + (rr * ADDS + ADD_RANK[uu] + 1))
                        slope = slopes[:, bass.ds(g * REP + r, 1)]
                        if u in (2, 3):
                            a = 256 if u == 2 else 0
                            pairs = [(probs[:, s, 0:512], far[:, a:a + 512], score_ps[:, c % 2, 0:512]),
                                     (probs[:, s, 512:1024], far[:, a + 128:a + 640], score_ps[:, c % 2, 512:1024])]
                        elif u == 1:
                            halves = [near[:, :], probs[:, s, 0:512], score_ps[:, c % 2, 0:512]]
                            n_, p_, s_ = (z.rearrange("p (a c) -> p a c", a=2) for z in halves)
                            pairs = [(p_, n_[:, :, 0:256], s_)]
                        else:
                            pairs = [(probs[:, s, :], near[:, :], score_ps[:, c % 2, :])]
                        for dst, reach, src in pairs:
                            last = v.scalar_tensor_tensor(out=dst, in0=reach, scalar=slope, in1=src,
                                                          op0=ALU.mult, op1=ALU.add)
                        last.then_inc(biased, 1)

                    def split(r, u):
                        c = r * NU + u
                        s, w = c % P_SLOTS, WIDTH[u]
                        dve.wait_ge(p_split_hi, it * UNITS_IT + (c + 1))
                        v.tensor_tensor(p_lo[:, s, 0:w], probs[:, s, 0:w], p_hi[:, s, 0:w].bitcast(F32), ALU.subtract
                                        ).then_inc(p_split_lo, 1)

                    def split_ctx(r, qc):
                        dve.wait_ge(ctx_split_hi, (it * REP + r) * QC + (qc + 1))
                        q = slice(qc * 512, (qc + 1) * 512)
                        v.tensor_tensor(ctx_lo[:, q], ctx_ps[:, qc, :], ctx_hi[:, q].bitcast(F32), ALU.subtract
                                        ).then_inc(ctx_split_lo, 1)

                    def invert(r):
                        dve.wait_ge(summed, it * REP + (r + 2))
                        v.reciprocal(rinv[:, :], work[:, JOBS.index(("sum", r)) % 2, 0:NT]).then_inc(inverted, 1)

                    def add_out(r, tiles):
                        if 0 in tiles:
                            dve.wait_ge(inverted, it * REP + (r + 1))
                        for t in tiles:
                            n = r * NT + t
                            dve.wait_ge(out_done, it * OUTS_IT + (n + 1))
                            dve.wait_ge(out_added, it * OUTS_IT + (max(n - NT + 1, 0) + 1))
                            v.scalar_tensor_tensor(out=x_tile(t), in0=work[:, JOBS.index(("out", n)) % 2, :],
                                                   scalar=rinv[:, t:t + 1], in1=x_tile(t), op0=ALU.mult, op1=ALU.add
                                                   ).then_inc(out_added, 1)

                    for n in range(4):
                        rotate(n)
                    for n in range(2):
                        dve.wait_ge(v_split_hi, it * 2 + (n + 1))
                        v.tensor_tensor(v_lo[:, n * 4:(n + 1) * 4, :].rearrange("p k d -> p (k d)"), work[:, n, :],
                                        v_hi[:, n * 4:(n + 1) * 4, :].rearrange("p k d -> p (k d)").bitcast(F32),
                                        ALU.subtract).then_inc(v_split_lo, 1)
                    dve.wait_ge(bias_added, b * NT + NT)
                    for r in range(REP):
                        bias(r, 0)
                        bias(r, 1)
                        if r:
                            invert(r - 1)
                            add_out(r - 1, (0, 1))
                        bias(r, 2)
                        if r:
                            add_out(r - 1, (2, 3))
                        split(r, 0)
                        if r:
                            add_out(r - 1, (4, 5))
                        split(r, 1)
                        bias(r, 3)
                        if r:
                            add_out(r - 1, (6, 7))
                        split(r, 2)
                        bias(r, 4)
                        if r < REP - 1:
                            rotate(4 + 2 * r)
                            rotate(5 + 2 * r)
                        split(r, 3)
                        split(r, 4)
                        split_ctx(r, 0)
                        split_ctx(r, 1)
                    invert(REP - 1)
                    add_out(REP - 1, range(NT))

            def apply_mask(n, s):
                dve.wait_ge(mask_in[s], n * 16 + 16)
                v.tensor_tensor(mask[:, s, :], mask[:, s, :], weight_t[:, :], ALU.mult).then_inc(weighted, 1)

            def add_y(n, s):
                dve.wait_ge(y_done, n * STEP + (s + 3))
                dve.wait_ge(y_out[s % ROWS], n * (16 * STEP // ROWS) + 16 * (s // ROWS + 1))
                v.tensor_tensor(y[s % ROWS][:, :], work[:, s % 2, :], row[s % ROWS][:, D:2 * D], ALU.add
                                ).then_inc(y_added, 1)

            dve.wait_ge(out_added, 1 + B * G * OUTS_IT)
            norm_stats(lambda t: acc[:, t, :], TILES, l2_step, l2_root, 0, 1)
            for t in range(TILES):
                v.tensor_scalar(xn[:, t, :], acc[:, t, :], mean_var[:, t, 0:1], rs[:, 2, t:t + 1],
                                ALU.subtract, ALU.mult).then_inc(l2_normed, 1)
            dve.wait_ge(l2_logits, TILES)
            v.tensor_copy(logits[:, :, :].rearrange("p t e -> p (t e)"), work[:, 1, :]).then_inc(l2_kept, 1)
            dve.wait_ge(l2_kept, 1)
            dve.wait_ge(consts2_in, 16 * CONSTS2)

            count = [0]

            def step(ins):
                count[0] += 1
                ins.then_inc(route, 1)
                dve.wait_ge(route, count[0])

            def over_experts(ap):
                return ap.rearrange("p (t a) -> p t a", a=1).to_broadcast([P, TILES, E])

            step(v.tensor_reduce(top[:, :], logits[:, :, :], AX.X, ALU.max))
            step(v.tensor_tensor(expo[:, :, :], logits[:, :, :], over_experts(top[:, :]), ALU.subtract))
            assert count[0] == SHIFTED
            step(v.tensor_tensor(one_hot[:, :, :], logits[:, :, :], over_experts(top[:, :]), ALU.is_equal))
            step(v.scalar_tensor_tensor(out=rank[:, :, :], in0=one_hot[:, :, :], scalar=float(-E),
                                        in1=expert_ids[:, :, :], op0=ALU.mult, op1=ALU.add))
            step(v.tensor_reduce(first[:, :], rank[:, :, :], AX.X, ALU.min))
            step(v.tensor_scalar(first[:, :], first[:, :], float(E), None, ALU.add))
            step(v.tensor_tensor(one_hot[:, :, :], expert_ids[:, :, :], over_experts(first[:, :]), ALU.is_equal))
            assert count[0] == HOT_KNOWN
            dve.wait_ge(route_exp, 1)
            step(v.tensor_reduce(top_w[:, 0, :], expo[:, :, :], AX.X, ALU.add))
            step(v.reciprocal(top_w[:, 1, :], top_w[:, 0, :]))
            step(v.memset(before[:, 0, :], 0.0))
            dve.wait_ge(ranked, 2)
            for t in range(TILES):
                step(v.tensor_tensor(before[:, t + 1, :], score_ps[:, 1, t * E:(t + 1) * E], before[:, t, :], ALU.add))
            step(v.tensor_scalar(more_tiles_i[:, 0, :], before[:, TILES, :], -1.0, 0.0, ALU.add, ALU.max))
            step(v.tensor_scalar(more_tiles_i[:, 1, :], more_tiles_i[:, 0, :], 7, None, ALU.logical_shift_right))
            step(v.tensor_copy(more_tiles[:, 0, :], more_tiles_i[:, 1, :]))
            step(v.tensor_tensor_scan(more_tiles[:, 1, :], ones[:, 0:E], more_tiles[:, 0, :], 0.0, ALU.mult, ALU.add))
            step(v.tensor_tensor(more_tiles[:, 2, :], more_tiles[:, 1, :], more_tiles[:, 0, :], ALU.subtract))
            step(v.tensor_tensor(rank[:, :, :].rearrange("p t e -> p (t e)"), score_ps[:, 0, 0:512],
                                 before[:, 0:TILES, :].rearrange("p t e -> p (t e)"), ALU.add))
            step(v.tensor_tensor(rank[:, :, :], rank[:, :, :], one_hot[:, :, :], ALU.mult))
            number, overflow_slot, own_slot = (slot_parts[:, i, :] for i in range(3))
            step(v.tensor_reduce(number, rank[:, :, :], AX.X, ALU.add))
            step(v.tensor_tensor(rank[:, :, :], more_tiles[:, 2:3, :].to_broadcast([P, TILES, E]), one_hot[:, :, :],
                                 ALU.mult))
            step(v.tensor_reduce(overflow_slot, rank[:, :, :], AX.X, ALU.add))
            step(v.tensor_scalar(own_slot, first[:, :], float(P), None, ALU.mult))
            step(v.tensor_scalar(overflow_slot, overflow_slot, float(P), float(P * (E - 1)), ALU.mult, ALU.add))
            step(v.tensor_tensor(overflow_slot, overflow_slot, own_slot, ALU.subtract))
            step(v.scalar_tensor_tensor(out=overflow_slot, in0=number, scalar=float(P), in1=overflow_slot,
                                        op0=ALU.is_ge, op1=ALU.mult))
            step(v.tensor_tensor(own_slot, own_slot, number, ALU.add))
            step(v.tensor_tensor(slot_i[:, :], own_slot, overflow_slot, ALU.add))
            assert count[0] == SLOTS_KNOWN, count[0]
            step(v.tensor_tensor(tile_past[:, :, :], tile_ids[:, :, :],
                                 more_tiles[0:1, 1:2, :].to_broadcast([1, OVERFLOW_TILES, E]), ALU.is_ge))
            step(v.tensor_reduce(tile_expert[:, :], tile_past[:, :, :], AX.X, ALU.add))
            step(v.tensor_scalar(tile_expert_i[:, :], tile_expert[:, :], float(E - 1), None, ALU.min))
            step(v.tensor_copy(overflow_i[:, :], more_tiles[0:1, 1, E - 1:E]))
            assert count[0] == EXPERTS_KNOWN, count[0]
            for t in range(TILES):
                v.tensor_scalar(xn[:, t, :], xn[:, t, :], top_w[:, 1, t:t + 1], None, ALU.mult).then_inc(rows_scaled, 1)
            step(v.tensor_scalar(weight_t[:, :], weight_t[:, :], 2.0, 1.0, ALU.mult, ALU.min))
            step(v.tensor_scalar(weight_t[:, :], weight_t[:, :], -1.0, ROUND, ALU.max, ALU.add))
            step(v.tensor_scalar(weight_t[:, :], weight_t[:, :], ROUND, None, ALU.subtract))
            w3 = weight_t[:, :].rearrange("p (c n) -> p c n", c=DC)
            step(v.tensor_tensor(w3, w3, scale_t[:, :].rearrange("p (a n) -> p a n", a=1).to_broadcast([P, DC, D]), ALU.mult))
            for s in range(STEP // 2):
                apply_mask(0, s)
            dve.wait_ge(slots_turned, 1)
            v.tensor_copy(slot_tok_i[:, :], ctx_ps[:, 0, 0:SLOT_TILES]).then_inc(slots_copied, 1)
            def expert_tiles(n, last):
                for s in range(STEP):
                    ahead = s + STEP // 2
                    if ahead < STEP:
                        apply_mask(n, ahead)
                    elif not last:
                        apply_mask(n + 1, ahead - STEP)
                    add_y(n, s)

            with dve.Fori(0, E // STEP - 1) as n:
                expert_tiles(n, False)
            expert_tiles(E // STEP - 1, True)
            with dve.If(dve.value_load(overflow_i[0:1, 0:1], min_val=0, max_val=OVERFLOW_TILES) > 0):
                with dve.Fori(0, OVERFLOW_TILES // STEP) as n:
                    for s in range(STEP):
                        apply_mask(n + E // STEP, s)
                        add_y(n + E // STEP, s)

        @block.gpsimd
        def _(pool):
            p = nc.gpsimd
            for s in (rope_lo, p_added, wo_split_lo):
                pool.sem_inc(s, 1)

            def split_wq():
                p.tensor_tensor(wq_lo[:, :, :].rearrange("p c n -> p (c n)"), wq_in[:, :],
                                wq_hi[:, :, :].rearrange("p c n -> p (c n)").bitcast(F32), ALU.subtract
                                ).then_inc(wq_split_lo, 1)

            def split_wkv():
                p.tensor_tensor(wkv_lo[:, :, :, :].rearrange("p a c n -> p (a c n)"), wkv_in[:, :],
                                wkv_hi[:, :, :, :].rearrange("p a c n -> p (a c n)").bitcast(F32), ALU.subtract
                                ).then_inc(wkv_split_lo, 1)

            pool.wait_ge(wq_split_hi, 1)
            split_wq()
            pool.wait_ge(wkv_split_hi, 1)
            split_wkv()
            pool.wait_ge(consts_in, 16 * CONSTS)
            with pool.Fori(0, B) as b:
                for t in range(NT):
                    pool.wait_ge(ln_normed, b * NT + (t + 1))
                    tile = acc[:, bass.ds(b * NT + t, 1), :].rearrange("p a n -> p (a n)")
                    p.tensor_tensor(tile, tile, bo_t[:, :], ALU.add).then_inc(bias_added, 1)
                with pool.Fori(0, G) as g:
                    it = b * G + g

                    def rope_add(n):
                        pool.wait_ge(rope_ready, it * ROPES_IT + (n + 1))
                        i = n % 2
                        p.tensor_tensor(rope_a[:, i, :], rope_a[:, i, :], rope_b[:, i, :], ALU.add).then_inc(rope_sum, 1)

                    def rope_split(n, dst, hi):
                        pool.wait_ge(rope_hi, it * ROPES_IT + (n + 1))
                        p.tensor_tensor(dst, rope_a[:, n % 2, :], hi.bitcast(F32), ALU.subtract).then_inc(rope_lo, 1)

                    def past_only(r, u):
                        c = r * NU + u
                        s = c % P_SLOTS
                        pool.wait_ge(exped, it * UNITS_IT + (c + 1))
                        pool.sem_inc(waited_pool, 1)
                        two = probs[:, s, 0:512 if u == 1 else 1024].rearrange("p (a c) -> p a c", a=2)[:, :, 0:P]
                        last = p.affine_select(out=two, in_=two, compare_op=ALU.is_ge, fill=0.0, base=0,
                                               pattern=[[0, 2], [1, P]], channel_multiplier=-1)
                        if u != 1:
                            one = probs[:, s, 896:1024]
                            last = p.affine_select(out=one, in_=one, compare_op=ALU.is_ge, fill=0.0, base=0,
                                                   pattern=[[1, P]], channel_multiplier=-1)
                        last.then_inc(masked, 1)
                        pool.wait_ge(masked, (it * REP + r) * MASKS + MASK_RANK[u])

                    def add_probs(r, k, q0, q1, a, b_=None):
                        done = (it * REP + r) * ADDS + k
                        pool.wait_ge(p_added, done)
                        if b_ is None:
                            p.tensor_tensor(psums[:, q0:q1], psums[:, q0:q1], a, ALU.add).then_inc(p_added, 1)
                        else:
                            p.tensor_tensor(psums[:, q0:q1], a, b_, ALU.add).then_inc(p_added, 1)

                    for n in range(4):
                        rope_add(n)
                        a = (n % 2) * 512
                        hi, lo = (q_hi[:, 0, a:a + 512], q_lo[:, 0, a:a + 512]) if n < 2 else \
                            (k_hi[:, a:a + 512], k_lo[:, a:a + 512])
                        rope_split(n, lo, hi)
                    for r in range(REP):
                        def pr(u, c0, c1):
                            return probs[:, (r * NU + u) % P_SLOTS, c0:c1]

                        past_only(r, 0)
                        pool.wait_ge(summed, it * REP + (r + 1))
                        add_probs(r, 1, P, 512, pr(0, P, 512), pr(0, 512, 896))
                        pool.wait_ge(p_added, (it * REP + r) * ADDS + 2)
                        p.tensor_tensor(psums[:, 0:P], pr(0, 0, P), ones[:, :], ALU.mult).then_inc(p_added, 1)
                        add_probs(r, 3, 384, 512, pr(0, 896, 1024))
                        past_only(r, 1)
                        add_probs(r, 4, 256, 512, pr(1, 0, 256))
                        pool.wait_ge(wq_split_hi, it * REP + (r + 2))
                        split_wq()
                        pool.wait_ge(exped, it * UNITS_IT + (r * NU + 3))
                        add_probs(r, 5, 512, 1024, pr(2, 0, 512), pr(2, 512, 1024))
                        add_probs(r, 6, 768, 1024, pr(1, 256, 512))
                        if r == 1:
                            pool.wait_ge(wkv_split_hi, it + 2)
                            split_wkv()
                        pool.wait_ge(exped, it * UNITS_IT + (r * NU + 4))
                        add_probs(r, 7, 512, 1024, pr(3, 0, 512))
                        add_probs(r, 8, 512, 1024, pr(3, 512, 1024))
                        n = 4 + 2 * r
                        if r < REP - 1:
                            rope_add(n)
                        past_only(r, 4)
                        if r < REP - 1:
                            rope_split(n, q_lo[:, (r + 1) % 2, 0:512], q_hi[:, (r + 1) % 2, 0:512])
                            rope_add(n + 1)
                            rope_split(n + 1, q_lo[:, (r + 1) % 2, 512:1024], q_hi[:, (r + 1) % 2, 512:1024])
                        add_probs(r, 9, 512, 1024, pr(4, 0, 512))
                        add_probs(r, 10, 640, 1024, pr(4, 512, 896))
                        add_probs(r, 11, 896, 1024, pr(4, 896, 1024))
                        pool.wait_ge(wo_split_hi, it * REP + (r + 2))
                        p.tensor_tensor(wo_lo[:, :], wo_in[:, :], wo_hi[:, :].bitcast(F32), ALU.subtract
                                        ).then_inc(wo_split_lo, 1)

            def store(s):
                p.indirect_dma_start(out_rows, bass.IndirectOffsetOnAxis(ap=out_idx[s][:, :], axis=0), y[s][:, :],
                                     None, bounds_check=B * T - 1, oob_is_err=False).then_inc(y_out[s], 16)

            pool.wait_ge(out_added, 1 + B * G * OUTS_IT)
            for s in range(ROWS):
                p.memset(row[s][:, :], 0.0).then_inc(rows_cleared, 1)
                p.memset(y[s][:, :], 0.0).then_inc(rows_cleared, 1)
                p.memset(out_idx[s][:, :], NO_TOKEN).then_inc(rows_cleared, 1)
            pool.wait_ge(rows_cleared, 3 * ROWS)
            for s in range(ROWS):
                store(s)
            pool.wait_ge(consts2_in, 16 * CONSTS2)
            pool.wait_ge(slots_cleared, 16)
            pool.wait_ge(route, SLOTS_KNOWN)
            for t in range(TILES):
                p.indirect_dma_start(slot_tokens_d, bass.IndirectOffsetOnAxis(ap=slot_i[:, t:t + 1], axis=0),
                                     token_ids[:, t:t + 1], None).then_inc(slots_written, 16)

            def set_index(idx, s, n, tile):
                p.tensor_copy(idx[s][:, :], slot_tok_i[:, bass.ds(n * STEP + tile, 1)]).then_inc(idx_set, 1)

            def gather(s):
                p.indirect_dma_start(row[s][:, :], None, rows_d, bass.IndirectOffsetOnAxis(ap=row_idx[s][:, :], axis=0),
                                     bounds_check=B * T - 1, oob_is_err=False).then_inc(row_in[s], 16)

            pool.wait_ge(slots_copied, 1)
            pool.wait_ge(x1_rows_out, 16)
            pool.wait_ge(xn_rows_out, 16)
            for s in range(ROWS):
                set_index(row_idx, s, 0, s)
                pool.wait_ge(idx_set, s + 1)
                gather(s)

            def expert_tiles(n, last):
                for s in range(STEP):
                    i = s % ROWS
                    landed = n * (16 * STEP // ROWS) + 16 * (s // ROWS + 1)
                    more = s + ROWS < STEP or not last
                    pool.wait_ge(y_out[i], landed)
                    pool.sem_inc(waited_pool, 1)
                    set_index(out_idx, i, n, s)
                    if more:
                        pool.wait_ge(row_in[i], landed)
                        pool.sem_inc(waited_pool, 1)
                        set_index(row_idx, i, n, s + ROWS)
                    pool.wait_ge(idx_set, n * (2 * STEP) + (ROWS + 2 * s + 2 if more else 2 * ROWS + s + 1))
                    pool.wait_ge(y_added, n * STEP + (s + 3))
                    pool.sem_inc(waited_pool, 1)
                    store(i)
                    if more:
                        gather(i)

            with pool.Fori(0, E // STEP - 1) as n:
                expert_tiles(n, False)
            expert_tiles(E // STEP - 1, True)
            with pool.If(pool.value_load(overflow_i[0:1, 0:1], min_val=0, max_val=OVERFLOW_TILES) > 0):
                with pool.Fori(0, OVERFLOW_TILES // STEP) as n:
                    for s in range(STEP):
                        i, m = s % ROWS, n + E // STEP
                        landed = m * (16 * STEP // ROWS) + 16 * (s // ROWS)
                        pool.wait_ge(y_out[i], landed + 16)
                        pool.wait_ge(row_in[i], landed)
                        pool.wait_ge(y_added, m * STEP + (s + 3 - ROWS))
                        pool.sem_inc(waited_pool, 1)
                        set_index(out_idx, i, m, s)
                        set_index(row_idx, i, m, s)
                        pool.wait_ge(idx_set, m * (2 * STEP) + (2 * s + 2))
                        pool.sem_inc(waited_pool, 1)
                        gather(i)
                        pool.wait_ge(y_added, m * STEP + (s + 3))
                        pool.sem_inc(waited_pool, 1)
                        store(i)
                for s in range(ROWS):
                    pool.wait_ge(y_out[s], 16 * (SLOT_TILES // ROWS) + 16)
                    pool.wait_ge(row_in[s], 16 * (SLOT_TILES // ROWS))
            for s in range(ROWS):
                pool.wait_ge(y_out[s], 16 * (E // ROWS) + 16)
                pool.wait_ge(row_in[s], 16 * (E // ROWS))


def tables():
    inv_freq = (np.float32(1.0) / np.float32(ROPE_THETA) ** (np.arange(0, DH, 2, dtype=np.float32) / np.float32(DH)))
    angle = (np.arange(T, dtype=np.float32)[:, None] * inv_freq[None, :].astype(np.float32)).T
    cosines = np.concatenate([np.cos(angle)] * 2).astype(np.float32)
    sines = np.concatenate([np.sin(angle), -np.sin(angle)]).astype(np.float32)
    key = np.arange(P, dtype=np.float32)[:, None]
    near = np.concatenate([np.arange(w) for w in (512, 384, 128)]).astype(np.float32)[None, :] - key
    far = np.arange(P, 1024, dtype=np.float32)[None, :] - key
    slopes = 2.0 ** (-np.arange(1, H + 1, dtype=np.float32) * np.float32(8.0 / H))
    spread = np.ones((P, 1), np.float32)
    experts = np.arange(E, dtype=np.float32)
    return {
        "cosines": cosines, "sines": sines, "negslopes": -spread * slopes[None, :].astype(np.float32),
        "reach_near": near, "reach_far": far, "ident_in": np.eye(P, dtype=np.float32),
        "earlier_in": np.triu(np.ones((P, P), np.float32), 1),
        "expert_ids_in": np.tile(experts, (P, TILES, 1)),
        "tile_ids_in": np.repeat(np.arange(OVERFLOW_TILES, dtype=np.float32), E).reshape(1, OVERFLOW_TILES, E),
        "token_ids_in": (np.arange(TILES) * P + np.arange(P)[:, None]).astype(np.float32),
        "no_tokens_in": np.full((P, SLOT_TILES), NO_TOKEN, np.float32),
    }


def kernel(**inputs):
    from concourse import bacc
    from concourse.bass_utils import run_bass_kernel_spmd

    a = {k.split("_", 2)[2]: np.ascontiguousarray(v) for k, v in inputs.items()}
    halves = np.concatenate([np.arange(0, DH, 2), np.arange(1, DH, 2)])

    def by_head(w, order=slice(None)):
        return w.reshape(DC, P, -1, DH)[..., order].transpose(2, 1, 0, 3).reshape(-1, P, DC * DH)

    wq = by_head(a["Wq"], halves)
    wkv = np.stack([by_head(a["Wk"], halves), by_head(a["Wv"])], axis=2).reshape(G, P, 2 * DC * DH)
    arrays = {
        "x": a["hidden_states"],
        "wq": np.concatenate([wq, wq[:1]]),
        "wkv": np.concatenate([wkv, wkv[:1]]),
        "wo": a["Wo"],
        "bo": np.tile(a["bo"], (P, 1)),
        "router": a["router_w"].T.reshape(DC, P, E).transpose(1, 0, 2),
        "weight": a["weight"].T.reshape(DC, P, D).transpose(1, 0, 2).reshape(P, DC * D),
        "scale": np.tile(a["scale"], (P, 1)),
        "masks": a["expert_masks"].transpose(0, 2, 1).reshape(E, DC, P, D).transpose(0, 2, 1, 3).reshape(E, P, DC * D),
        **tables(),
    }
    arrays = {f"{k}_dram": np.ascontiguousarray(v) for k, v in arrays.items()}
    nc = bacc.Bacc("TRN2", target_bir_lowering=False, num_devices=1)
    args = {k[:-5]: nc.dram_tensor(k, v.shape, mybir.dt.from_np(v.dtype), kind="ExternalInput").ap()
            for k, v in arrays.items()}
    args["rows_d"] = nc.dram_tensor("rows_scratch", (B * T, 2 * D), F32, kind="Internal").ap()
    args["slot_tokens_d"] = nc.dram_tensor("slot_tokens_scratch", (SLOT_TILES * P, 1), F32, kind="Internal").ap()
    args["out"] = nc.dram_tensor("out_dram", (B, T, D), F32, kind="ExternalOutput").ap()
    block_kernel(nc, **args)
    r = run_bass_kernel_spmd(nc, [arrays], core_ids=[0])
    return r.results[0]["out_dram"]
```

```python
from contextlib import ExitStack

import numpy as np

import concourse.bass as bass
from concourse import mybir

ALU = mybir.AluOpType
ACT = mybir.ActivationFunctionType
AX = mybir.AxisListType
F32 = mybir.dt.float32
F32R = mybir.dt.float32r
I32 = mybir.dt.int32
U32 = mybir.dt.uint32

P = 128
B, T, D = 2, 1024, 512
H, G, DH = 16, 4, 128
REP = H // G
E = 32
NT = T // P
TILES = B * NT
DC = D // P
QC = T // 512
LN_EPS = 1e-5
ROPE_THETA = 10000.0
TANH_CAP = 30.0
OVERFLOW_TILES = TILES
SLOT_TILES = E + OVERFLOW_TILES
STEP, ROWS, YS = 16, 8, 4
NO_TOKEN = 2 * B * T
ROUND = 1.5 * 2.0 ** 23

UNITS = [
    [(0, 0, 0, 512, 0), (1, 0, 128, 384, 512), (3, 0, 384, 128, 896)],
    [(2, 0, 256, 256, 0), (6, 1, 256, 256, 256)],
    [(1, 1, 0, 512, 0), (0, 1, 0, 512, 512)],
    [(3, 1, 0, 512, 0), (2, 1, 0, 512, 512)],
    [(4, 1, 0, 512, 0), (5, 1, 128, 384, 512), (7, 1, 384, 128, 896)],
]
NU = len(UNITS)
WIDTH = [sum(e[3] for e in u) for u in UNITS]
DIAGONAL = [True, True, False, False, True]
ADDS = 11
ADD_RANK = [3, 6, 5, 8, 11]
MASKS = 3
MASK_RANK = [1, 2, None, None, 3]
UNITS_IT = REP * NU
P_SLOTS = 4
LAG = 2
ROPES_IT = 2 * REP + 2
OUTS_IT = REP * NT
W_IT = REP + 2
W_Q, W_K, W_V = (0, 2, 4, 5), 1, 3
LN_STEPS = 2 * NT + 5
CONSTS = 6
CONSTS2 = 5
SHIFTED, HOT_KNOWN, SLOTS_KNOWN, EXPERTS_KNOWN = 2, 7, 42, 46


def steps(r, more=True):
    first_of_group, last_of_group = r % REP == 0, r == REP - 1
    q = [[("q", n)] if more or not last_of_group else [] for n in range(2)]
    k = [[("k", n)] if more and last_of_group else [] for n in range(2)]
    v = [("v", 0), ("v", 1)] if first_of_group else []
    vt = [("vt", 0), ("vt", 1)] if first_of_group else []
    o = [[("out", t)] if r else [] for t in range(NT)]
    total = [("sum", 0)] if r else []
    scores = [[("qk", u)] for u in range(NU)]
    context = [[("pv", u - LAG)] if r or u >= LAG else [] for u in range(NU)]
    start = q[0] + scores[0] if first_of_group else scores[0] + q[0]
    return (start + context[0]
            + scores[1] + q[1] + context[1] + v + vt
            + scores[2] + total + o[0] + k[0] + context[2] + o[1]
            + scores[3] + o[2] + k[1] + context[3] + o[3]
            + scores[4] + o[4] + o[5] + context[4] + o[6] + o[7])


DRAIN = [("pv", u - LAG) for u in range(LAG)] + [("sum", 0)] + [("out", t) for t in range(NT)]


def bank_jobs(parts):
    jobs = [(r, *step) for r, part in parts for step in part if step[0] not in ("qk", "pv")]
    return {job: i for i, job in enumerate(jobs)}


START = bank_jobs([(-1, [("q", 0), ("q", 1), ("k", 0), ("k", 1)]), (0, steps(0))])
GROUP = bank_jobs([(r, steps(r)) for r in range(1, REP + 1)])
END = bank_jobs([(r, steps(r, False)) for r in range(1, REP)] + [(REP, DRAIN)])
JOBS_BATCH = len(START) + (G - 1) * len(GROUP) + len(END)
assert len(START) % 2 == len(GROUP) % 2 == len(END) % 2 == 0
JOBS_DONE = 2 + B * JOBS_BATCH


def next_rope(r, kind, n):
    group, head = divmod(r + 1, REP)
    return group * ROPES_IT + (2 + n if kind == "k" else (2 + 2 * head if head else 0) + n)


def block_kernel(nc, x, w, wo, bo, cosines, sines, negslopes, reach_near, reach_far, ident_in, earlier_in,
                 expert_ids_in, tile_ids_in, tokens_in, no_tokens_in, router, weight, scale,
                 masks, rows_d, slot_tokens_d, out):
    ctx = ExitStack()
    with ctx:
        attn = ExitStack()

        def sb(name, shape, dt=F32, stack=ctx):
            return stack.enter_context(nc.sbuf_tensor(name, shape, dt))

        def asb(name, shape, dt=F32):
            return sb(name, shape, dt, attn)

        def sem(name):
            return ctx.enter_context(nc.semaphore(name))

        acc = sb("acc", [P, TILES, D])
        ident = sb("ident", [P, P])
        ones = sb("ones", [P, P])
        mean_var = sb("mean_var", [P, TILES, 2])
        stats = sb("stats", [P, TILES, 6])
        stats2 = sb("stats2", [P, TILES, 6])
        rs = sb("rs", [P, 4, TILES])

        xt_hi = asb("xt_hi", [P, DC, T], F32R)
        xt_lo = asb("xt_lo", [P, DC, T], F32R)
        k_hi = asb("k_hi", [P, T], F32R)
        k_lo = asb("k_lo", [P, T], F32R)
        v_hi = asb("v_hi", [P, NT, DH], F32R)
        v_lo = asb("v_lo", [P, NT, DH], F32R)
        q_hi = asb("q_hi", [P, 2, T], F32R)
        q_lo = asb("q_lo", [P, 2, T], F32R)
        probs = asb("probs", [P, P_SLOTS, 1024])
        p_hi = asb("p_hi", [P, P_SLOTS, 1024], F32R)
        p_lo = asb("p_lo", [P, P_SLOTS, 1024], F32R)
        psums = asb("psums", [P, 2, T])
        ctx_hi = asb("ctx_hi", [P, T], F32R)
        ctx_lo = asb("ctx_lo", [P, T], F32R)
        rinv = asb("rinv", [P, NT])
        w_in = asb("w_in", [P, DC * DH])
        w_hi = asb("w_hi", [P, 2, DC, DH], F32R)
        w_lo = asb("w_lo", [P, 2, DC, DH], F32R)
        wo_in = asb("wo_in", [P, D])
        wo_hi = asb("wo_hi", [P, D], F32R)
        wo_lo = asb("wo_lo", [P, D], F32R)
        cos_t = asb("cos_t", [P, T])
        sin_t = asb("sin_t", [P, T])
        rope_a = asb("rope_a", [P, 2, 512])
        xnorm = probs[:, :, 0:D]
        rope_b = asb("rope_b", [P, 2, 512])
        bo_t = asb("bo_t", [P, D])
        slopes = asb("slopes", [P, H])
        far = asb("far", [P, 7 * P])
        near = asb("near", [P, 1024])
        attn.close()

        xn = sb("xn", [P, TILES, D])
        router_t = sb("router_t", [P, DC, E])
        logits = sb("logits", [P, TILES, E])
        expo = sb("expo", [P, TILES, E])
        top = sb("top", [P, TILES])
        first = sb("first", [P, TILES])
        top_sum = sb("top_sum", [P, TILES])
        expert_ids = sb("expert_ids", [P, TILES, E])
        one_hot = sb("one_hot", [P, TILES, E])
        rank = sb("rank", [P, TILES, E])
        before = sb("before", [P, TILES + 1, E])
        earlier = sb("earlier", [P, P])
        more_tiles = sb("more_tiles", [P, 3, E])
        more_tiles_i = sb("more_tiles_i", [P, 2, E], I32)
        slot_parts = sb("slot_parts", [P, 3, TILES])
        slot_f = sb("slot_f", [P, TILES])
        slot_i = sb("slot_i", [P, TILES], U32)
        tokens = sb("tokens", [P, TILES, 2])
        tile_ids = sb("tile_ids", [1, OVERFLOW_TILES, E])
        tile_past = sb("tile_past", [1, OVERFLOW_TILES, E])
        tile_expert = sb("tile_expert", [1, OVERFLOW_TILES])
        tile_expert_i = sb("tile_expert_i", [1, OVERFLOW_TILES], I32)
        overflow_i = sb("overflow_i", [1, 1], I32)
        slot_rows = sb("slot_rows", [SLOT_TILES, P, 2])
        slot_weight = sb("slot_weight", [P, SLOT_TILES])
        slot_tok_i = sb("slot_tok_i", [P, SLOT_TILES], U32)
        weight_t = sb("weight_t", [P, DC * D])
        scale_t = sb("scale_t", [P, D])
        mask = sb("mask", [P, STEP // 2, DC * D])
        mask_buffer = [mask[:, i, :] for i in range(STEP // 2)]
        for rows in (xn, acc):
            mask_buffer += [rows[:, DC * i:DC * (i + 1), :].rearrange("p t n -> p (t n)") for i in range(STEP // 4)]
        rows_in = sb("rows_in", [P, ROWS, 2 * D])
        row = [rows_in[:, i, :] for i in range(ROWS)]
        xn_t = rows_in[:, 0:4, :].rearrange("p (q a) (i n) -> p q (a i) n", q=2, i=2)
        logits_t = rows_in[0:E, 4, :].rearrange("p (q n) -> p q n", q=2)
        row_t = sb("row_t", [P, 2, D])
        row_idx = [sb(f"row_idx{i}", [P, 1], U32) for i in range(ROWS)]
        out_idx = [sb(f"out_idx{i}", [P, 1], U32) for i in range(YS)]
        y = [sb(f"y{i}", [P, D]) for i in range(YS)]

        score_ps = ctx.enter_context(nc.psum_tensor("score_ps", [P, 2, 1024], F32))
        ctx_ps = ctx.enter_context(nc.psum_tensor("ctx_ps", [P, 2, 512], F32))
        work = ctx.enter_context(nc.psum_tensor("work", [P, 2, 512], F32))

        consts_in, ident_in_place = sem("consts_in"), sem("ident_in_place")
        x_in = [sem(f"x_in{i}") for i in range(NT // 2)]
        w_landed, wo_landed = sem("w_landed"), sem("wo_landed")
        w_split_hi, w_split_lo = sem("w_split_hi"), sem("w_split_lo")
        wo_split_hi, wo_split_lo = sem("wo_split_hi"), sem("wo_split_lo")
        ones_set = sem("ones_set")
        ln_step, ln_root, ln_normed = sem("ln_step"), sem("ln_root"), sem("ln_normed")
        ln_turned, ln_hi, ln_lo = sem("ln_turned"), sem("ln_hi"), sem("ln_lo")
        read_out = sem("read_out")
        bias_added = sem("bias_added")
        projected = sem("projected")
        rope_sum, rope_hi, rope_lo = sem("rope_sum"), sem("rope_hi"), sem("rope_lo")
        v_turned, v_split_hi = sem("v_turned"), sem("v_split_hi")
        scored, biased, tanhed, exped, masked = (sem("scored"), sem("biased"), sem("tanhed"), sem("exped"),
                                                 sem("masked"))
        p_split_hi, p_split_lo, p_added = sem("p_split_hi"), sem("p_split_lo"), sem("p_added")
        pv_done = sem("pv_done")
        ctx_split_hi, ctx_split_lo = sem("ctx_split_hi"), sem("ctx_split_lo")
        summed = sem("summed")
        out_done = sem("out_done")
        consts2_in = sem("consts2_in")
        l2_step, l2_root, l2_normed = sem("l2_step"), sem("l2_root"), sem("l2_normed")
        l2_turned, l2_copied = sem("l2_turned"), sem("l2_copied")
        l2_logits_t, l2_logits_kept = sem("l2_logits_t"), sem("l2_logits_kept")
        l2_logits, l2_kept = sem("l2_logits"), sem("l2_kept")
        route, route_exp, ranked = sem("route"), sem("route_exp"), sem("ranked")
        x1_rows_out, xn_rows_out = sem("x1_rows_out"), sem("xn_rows_out")
        slots_cleared, slots_written, slots_back = sem("slots_cleared"), sem("slots_written"), sem("slots_back")
        slots_turned = sem("slots_turned")
        weight_in, weight_step = sem("weight_in"), sem("weight_step")
        slots_copied, rows_cleared = sem("slots_copied"), sem("rows_cleared")
        mask_in = [sem(f"mask_in{i}") for i in range(STEP)]
        row_in = [sem(f"row_in{i}") for i in range(ROWS)]
        weighted, idx_set = sem("weighted"), sem("idx_set")
        rows_turned, rows_copied, y_done, y_added = sem("rows_turned"), sem("rows_copied"), sem("y_done"), sem("y_added")
        y_out = [sem(f"y_out{i}") for i in range(YS)]
        waited_dve, waited_pool = sem("waited_dve"), sem("waited_pool")

        out_rows = out.rearrange("b t n -> (b t) n")
        x_rows = x.rearrange("b (t p) n -> b p t n", p=P)
        wo_rows = wo.rearrange("(h d) n -> h d n", d=DH)
        rows_tiled = rows_d.rearrange("(t p) n -> p t n", p=P)

        block = ctx.enter_context(nc.Block())

        @block.sync
        def _(sp):
            def load_w(it, g, k):
                sp.wait_ge(w_split_lo, it * W_IT + (k + 1))
                sp.dma_start(w_in[:, :], w[bass.ds(g * W_IT + k, 1)].rearrange("a p n -> (a p) n")).then_inc(w_landed, 16)

            for i in range(NT // 2):
                sp.dma_start(acc[:, 2 * i:2 * i + 2, :], x_rows[0, :, 2 * i:2 * i + 2]).then_inc(x_in[i], 16)
            sp.dma_start(slot_tokens_d.rearrange("(p t) o -> p (t o)", p=P), no_tokens_in
                         ).then_inc(slots_cleared, 16)

            def load_wo(it, g, r):
                sp.wait_ge(wo_split_lo, it * REP + (r + 1))
                sp.dma_start(wo_in[:, :], wo_rows[bass.ds(g * REP + r, 1)].rearrange("a p n -> (a p) n")
                             ).then_inc(wo_landed, 16)

            def head(it, g, r, more=True):
                first = r // REP * W_IT
                if r % REP == 0:
                    load_w(it, g, first + 4)
                if r == 1 and more:
                    load_w(it, g, W_IT)
                load_wo(it, g, r)
                if r % REP == 0:
                    load_w(it, g, first + 5)
                elif more:
                    load_w(it, g, W_IT + r)

            with sp.Fori(0, B) as b:
                for k in range(4):
                    load_w(b * G, b * 0, k)
                head(b * G, b * 0, 0)
                with sp.Fori(0, G - 1) as g:
                    for r in range(1, REP):
                        head(b * G + g, g, r)
                    head(b * G + g, g, REP)
                for r in range(1, REP):
                    head(b * G + (G - 1), b * 0 + (G - 1), r, False)
                sp.wait_ge(read_out, b * JOBS_BATCH + (JOBS_BATCH + 2))
                sp.dma_start(rows_tiled[:, bass.ds(b * NT, NT), D:2 * D], acc[:, bass.ds(b * NT, NT), :]
                             ).then_inc(x1_rows_out, 16)
            sp.wait_ge(read_out, JOBS_DONE)
            for dst, src in ((router_t[:, :, :], router), (expert_ids[:, :, :], expert_ids_in),
                             (earlier[:, :], earlier_in), (tokens[:, :, :], tokens_in),
                             (tile_ids[:, :, :], tile_ids_in)):
                sp.dma_start(dst, src).then_inc(consts2_in, 16)
            sp.dma_start(scale_t[:, :], scale).then_inc(weight_in, 16)
            sp.dma_start(weight_t[:, :], weight).then_inc(weight_in, 16)
            for s in range(STEP // 2):
                sp.dma_start(mask_buffer[s], masks[s]).then_inc(mask_in[s], 16)
            sp.wait_ge(l2_normed, TILES)
            sp.dma_start(rows_tiled[:, :, 0:D], xn[:, :, :]).then_inc(xn_rows_out, 16)
            sp.wait_ge(xn_rows_out, 16)
            sp.wait_ge(l2_turned, TILES)
            sp.wait_ge(x1_rows_out, 16 * B)
            for s in range(STEP // 2, STEP - 2):
                sp.dma_start(mask_buffer[s], masks[s]).then_inc(mask_in[s], 16)
            sp.wait_ge(slots_written, 16 * TILES)
            sp.dma_start(slot_rows[:, :, :], slot_tokens_d.rearrange("(t p) o -> t p o", p=P)).then_inc(slots_back, 16)
            sp.wait_ge(row_in[ROWS - 1], 16)
            for s in range(STEP - 2, STEP):
                sp.dma_start(mask_buffer[s], masks[s]).then_inc(mask_in[s], 16)
            with sp.Fori(0, E // STEP - 1) as n:
                for s in range(STEP):
                    sp.wait_ge(y_done, n * STEP + (s + 3))
                    sp.dma_start(mask_buffer[s], masks[bass.ds(n * STEP + (s + STEP), 1)].rearrange("a p n -> (a p) n")
                                 ).then_inc(mask_in[s], 16)
            sp.wait_ge(route, EXPERTS_KNOWN)
            with sp.If(sp.value_load(overflow_i[0:1, 0:1], min_val=0, max_val=OVERFLOW_TILES) > 0):
                with sp.Fori(0, OVERFLOW_TILES // STEP) as n:
                    for s in range(STEP):
                        sp.wait_ge(y_done, n * STEP + (E - STEP + s + 3))
                        e = sp.value_load(tile_expert_i[0:1, bass.ds(n * STEP + s, 1)], min_val=0, max_val=E - 1)
                        sp.dma_start(mask_buffer[s], masks[bass.ds(e, 1)].rearrange("a p n -> (a p) n")
                                     ).then_inc(mask_in[s], 16)

        @block.tensor
        def _(pe):
            mm = nc.tensor.matmul

            def product(dst, lhs, rhs, first=True, last=True, skip=False):
                (lh, ll), (rh, rl) = lhs, rhs
                mm(dst, lh, rh, start=first, stop=False, skip_group_check=skip)
                mm(dst, lh, rl, start=False, stop=False, skip_group_check=skip)
                return mm(dst, ll, rh, start=False, stop=last, skip_group_check=skip)

            for s, n in ((pv_done, 4), (summed, 2), (projected, 4), (out_done, NT), (y_done, 2)):
                pe.sem_inc(s, n)
            pe.wait_ge(ident_in_place, 16)
            pe.wait_ge(ones_set, 1)

            def bank(jobs, i):
                pe.wait_ge(read_out, jobs + (i + 1))
                return work[:, i % 2, :]

            def project_t(it, w, jobs, i, n):
                pe.wait_ge(w_split_lo, it * W_IT + (w + 2))
                dst = bank(jobs, i)
                for c in range(DC):
                    last = product(dst, (w_hi[:, w % 2, c, :], w_lo[:, w % 2, c, :]),
                                   (xt_hi[:, c, n * 512:(n + 1) * 512], xt_lo[:, c, n * 512:(n + 1) * 512]),
                                   c == 0, c == DC - 1)
                last.then_inc(projected, 1)

            def turn_v(r, jobs, i, n, place):
                dst = bank(jobs, i)
                pe.wait_ge(read_out, jobs + (place[(r, "v", n)] + 3))
                for k in range(4):
                    last = nc.tensor.transpose(dst[:, k * P:(k + 1) * P], rope_b[:, n, k * P:(k + 1) * P], ident[:, :])
                last.then_inc(v_turned, 1)

            def score(it, r, u):
                c = r * NU + u
                rope = next_rope(r - 1, "q", 1)
                if r % REP == 0:
                    rope = next_rope(r - 1, "k", min(u, 1))
                pe.wait_ge(rope_lo, it * ROPES_IT + (rope + 3))
                pe.wait_ge(biased, it * UNITS_IT + (c + 1))
                for kt, qc, q0, w, col in UNITS[u]:
                    k = slice(kt * P, (kt + 1) * P)
                    q = slice(qc * 512 + q0, qc * 512 + q0 + w)
                    last = product(score_ps[:, c % 2, col:col + w], (k_hi[:, k], k_lo[:, k]),
                                   (q_hi[:, r % 2, q], q_lo[:, r % 2, q]))
                last.then_inc(scored, 1)

            def apply_v(it, c):
                r, u = divmod(c, NU)
                s = c % P_SLOTS
                pe.wait_ge(p_split_lo, it * UNITS_IT + (c + 1))
                if u < 2:
                    pe.wait_ge(ctx_split_lo, (it * REP + r) * QC + (u + 1))
                for kt, qc, q0, w, col in UNITS[u]:
                    last = product(ctx_ps[:, qc, q0:q0 + w], (v_hi[:, kt, :], v_lo[:, kt, :]),
                                   (p_hi[:, s, col:col + w], p_lo[:, s, col:col + w]),
                                   kt == (6 if qc else 0), kt == (7 if qc else 2), skip=True)
                last.then_inc(pv_done, 1)

            def sum_probs(it, r, jobs, i):
                pe.wait_ge(p_added, (it * REP + r) * ADDS + ADDS)
                dst = bank(jobs, i)
                for t in range(NT):
                    last = mm(dst[:, t:t + 1], psums[:, (r - 1) % 2, t * P:(t + 1) * P], ones[:, 0:1],
                              start=True, stop=True)
                last.then_inc(summed, 1)

            def project_out(it, r, jobs, i, t):
                if t % 4 == 0:
                    pe.wait_ge(ctx_split_lo, (it * REP + r) * QC + (t // 4 + 1))
                    pe.wait_ge(wo_split_lo, it * REP + (r + 1))
                dst = bank(jobs, i)
                q = slice(t * P, (t + 1) * P)
                product(dst, (ctx_hi[:, q], ctx_lo[:, q]), (wo_hi[:, :], wo_lo[:, :])).then_inc(out_done, 1)

            def work_through(it, r, todo, jobs, place):
                for kind, n in todo:
                    i = place.get((r, kind, n))
                    if kind == "qk":
                        score(it, r, n)
                    elif kind == "pv":
                        if r % REP == 0 and n in (0, 1):
                            pe.wait_ge(read_out, jobs + (place[(r, "vt", n)] + 3))
                        apply_v(it, r * NU + n)
                    elif kind == "q":
                        project_t(it, (r + 1) // REP * W_IT + W_Q[(r + 1) % REP], jobs, i, n)
                    elif kind == "k":
                        project_t(it, W_IT + W_K, jobs, i, n)
                    elif kind == "v":
                        project_t(it, r // REP * W_IT + W_V, jobs, i, n)
                    elif kind == "vt":
                        turn_v(r, jobs, i, n, place)
                    elif kind == "sum":
                        sum_probs(it, r, jobs, i)
                    else:
                        project_out(it, r, jobs, i, n)

            with pe.Fori(0, B) as b:
                jobs = b * JOBS_BATCH
                for t in range(NT):
                    pe.wait_ge(ln_normed, b * NT + (t + 1))
                    pe.wait_ge(ln_lo, b * NT + (t + 1))
                    for c in range(DC):
                        last = nc.tensor.transpose(score_ps[:, t % 4 // 2, t % 2 * D + c * P:t % 2 * D + (c + 1) * P],
                                                   xnorm[:, t % 4, c * P:(c + 1) * P], ident[:, :])
                    last.then_inc(ln_turned, 1)
                pe.wait_ge(ln_lo, b * NT + (NT + 4))
                for w in (W_Q[0], W_K):
                    for n in range(2):
                        project_t(b * G, w, jobs, START[(-1, "k" if w else "q", n)], n)
                work_through(b * G, 0, steps(0), jobs, START)
                with pe.Fori(0, G - 1) as g:
                    for r in range(1, REP + 1):
                        work_through(b * G + g, r, steps(r), b * JOBS_BATCH + g * len(GROUP) + len(START), GROUP)
                for r in range(1, REP):
                    work_through(b * G + (G - 1), r, steps(r, False), b * JOBS_BATCH + (JOBS_BATCH - len(END)), END)
                work_through(b * G + (G - 1), REP, DRAIN, b * JOBS_BATCH + (JOBS_BATCH - len(END)), END)

            pe.wait_ge(consts2_in, 16 * CONSTS2)
            pe.wait_ge(read_out, JOBS_DONE)

            def turn_xn(t):
                pe.wait_ge(l2_normed, t + 1)
                if t > 3:
                    pe.wait_ge(l2_copied, t - 3)
                for c in range(DC):
                    last = nc.tensor.transpose(score_ps[:, t % 4 // 2, t % 2 * D + c * P:t % 2 * D + (c + 1) * P],
                                               xn[:, t, c * P:(c + 1) * P], ident[:, :])
                last.then_inc(l2_turned, 1)

            def turn_logits(q):
                pe.wait_ge(l2_logits_kept, q + 1)
                for i in range(4):
                    t = q * 4 + i
                    last = nc.tensor.transpose(work[:, 1, t * E:(t + 1) * E], logits_t[:, q % 2, i * P:(i + 1) * P],
                                               ident[0:E, 0:E])
                last.then_inc(l2_logits, 1)

            for q in range(TILES // 4):
                for t in range(q * 4, q * 4 + 4):
                    turn_xn(t)
                if q:
                    turn_logits(q - 1)
                pe.wait_ge(l2_copied, q * 4 + 4)
                for c in range(DC):
                    last = mm(work[0:E, 0, :], router_t[:, c, :], xn_t[:, q % 2, :, c * P:(c + 1) * P],
                              start=c == 0, stop=c == DC - 1)
                last.then_inc(l2_logits_t, 1)
            turn_logits(TILES // 4 - 1)
            pe.wait_ge(route, HOT_KNOWN)
            hot = one_hot[:, :, :].rearrange("p t e -> p (t e)")
            mm(score_ps[:, 0, 0:512], earlier[:, :], hot, start=True, stop=True).then_inc(ranked, 1)
            mm(score_ps[:, 1, 0:512], ones[:, :], hot, start=True, stop=True).then_inc(ranked, 1)
            pe.wait_ge(slots_back, 16)
            for i in range(2):
                nc.tensor.transpose(ctx_ps[:, 0, i * SLOT_TILES:(i + 1) * SLOT_TILES], slot_rows[:, :, i],
                                    ident[0:SLOT_TILES, 0:SLOT_TILES]).then_inc(slots_turned, 1)

            def turn_rows(n, s):
                pe.wait_ge(row_in[s % ROWS], n * (16 * STEP // ROWS) + 16 * (s // ROWS + 1))
                for c in range(DC):
                    last = nc.tensor.transpose(ctx_ps[:, s % 2, c * P:(c + 1) * P],
                                               row[s % ROWS][:, c * P:(c + 1) * P], ident[:, :])
                last.then_inc(rows_turned, 1)

            def multiply(n, s):
                pe.wait_ge(rows_copied, n * STEP + (s + 2))
                pe.wait_ge(weighted, n * STEP + (s + 1))
                pe.wait_ge(y_added, n * STEP + (s + 1))
                for c in range(DC):
                    last = mm(work[:, s % 2, :], row_t[:, s % 2, c * P:(c + 1) * P], mask_buffer[s][:, c * D:(c + 1) * D],
                              start=c == 0, stop=c == DC - 1)
                last.then_inc(y_done, 1)

            def expert_tiles(n, last):
                for s in range(STEP):
                    if s < STEP - 1 or not last:
                        pe.wait_ge(rows_copied, n * STEP + (s + 1))
                        turn_rows(n if s < STEP - 1 else n + 1, (s + 1) % STEP)
                    multiply(n, s)

            pe.wait_ge(slots_copied, 2)
            turn_rows(0, 0)
            with pe.Fori(0, E // STEP - 1) as n:
                expert_tiles(n, False)
            expert_tiles(E // STEP - 1, True)
            pe.wait_ge(route, EXPERTS_KNOWN)
            with pe.If(pe.value_load(overflow_i[0:1, 0:1], min_val=0, max_val=OVERFLOW_TILES) > 0):
                with pe.Fori(0, OVERFLOW_TILES // STEP) as n:
                    for s in range(STEP):
                        pe.wait_ge(rows_copied, n * STEP + (E + s))
                        turn_rows(n + E // STEP, s)
                        multiply(n + E // STEP, s)

        @block.scalar
        def _(act):
            f = nc.scalar.activation
            act.sem_inc(rows_copied, 1)
            nc.scalar.dma_start(ident[:, :], ident_in).then_inc(ident_in_place, 16)
            for dst, src in ((cos_t, cosines), (sin_t, sines), (bo_t, bo), (slopes, negslopes), (near, reach_near),
                             (far, reach_far)):
                nc.scalar.dma_start(dst[:, :], src).then_inc(consts_in, 16)
            for i in range(NT // 2):
                act.wait_ge(x_in[i], 16)
                nc.scalar.dma_start(acc[:, NT + 2 * i:NT + 2 * i + 2, :], x_rows[1, :, 2 * i:2 * i + 2]
                                    ).then_inc(x_in[i], 16)

            def split_w(it, k):
                act.wait_ge(w_landed, it * (16 * W_IT) + 16 * (k + 1))
                act.wait_ge(projected, it * (2 * W_IT) + (2 * k + 2))
                f(w_hi[:, k % 2, :, :].rearrange("p c n -> p (c n)"), w_in[:, :], ACT.Copy).then_inc(w_split_hi, 1)

            def split_wo(it, r):
                act.wait_ge(wo_landed, (it * REP + r) * 16 + 16)
                act.wait_ge(out_done, (it * REP + r) * NT + NT)
                f(wo_hi[:, :], wo_in[:, :], ACT.Copy).then_inc(wo_split_hi, 1)

            def split_rope(it, r, kind, n):
                act.wait_ge(rope_sum, it * ROPES_IT + (next_rope(r, kind, n) + 1))
                dst = k_hi if kind == "k" else q_hi[:, (r + 1) % 2]
                f(dst[:, n * 512:(n + 1) * 512], rope_a[:, n, :], ACT.Copy).then_inc(rope_hi, 1)

            def tanh_exp(it, c):
                s, w = c % P_SLOTS, WIDTH[c % NU]
                act.wait_ge(biased, it * UNITS_IT + (c + 3))
                f(probs[:, s, 0:w], probs[:, s, 0:w], ACT.Tanh, scale=1.0 / (TANH_CAP * DH ** 0.5)
                  ).then_inc(tanhed, 1)
                act.wait_ge(tanhed, it * UNITS_IT + (c + 1))
                f(probs[:, s, 0:w], probs[:, s, 0:w], ACT.Exp, scale=TANH_CAP).then_inc(exped, 1)

            def split(it, c):
                r, u = divmod(c, NU)
                s, w = c % P_SLOTS, WIDTH[u]
                act.wait_ge(exped, it * UNITS_IT + (c + 1))
                if MASK_RANK[u]:
                    act.wait_ge(masked, (it * REP + r) * MASKS + MASK_RANK[u])
                f(p_hi[:, s, 0:w], probs[:, s, 0:w], ACT.Copy).then_inc(p_split_hi, 1)

            def split_ctx(it, c):
                r, qc = c // NU, 0 if c % NU == 1 else 1
                act.wait_ge(pv_done, it * UNITS_IT + (c + 5))
                act.wait_ge(out_done, (it * REP + r) * NT + (4 * qc + 4))
                f(ctx_hi[:, qc * 512:(qc + 1) * 512], ctx_ps[:, qc, :], ACT.Copy).then_inc(ctx_split_hi, 1)

            def work_through(it, r, todo, jobs, place, more=True):
                first = r // REP * W_IT
                for kind, n in todo:
                    c = r * NU + n
                    if kind == "qk":
                        if c:
                            split(it, c - 1)
                        if n == NU - 1 and r == REP - 1 and more:
                            act.wait_ge(scored, it * UNITS_IT + (c + 1))
                            for i in range(2):
                                split_rope(it, r, "k", i)
                        tanh_exp(it, c)
                        if n == 0 and r % REP == 0:
                            split_w(it, first + W_V)
                        if n == 1 and r:
                            split_wo(it, r - 1)
                        if n in (1, 2) and (more or r < REP - 1):
                            split_rope(it, r, "q", n - 1)
                        if n == 2 and r % REP == 0:
                            split_w(it, first + 4)
                        elif n == 2 and more:
                            split_w(it, first + W_IT + r % REP - 1)
                        if n == 4 and r % REP == 0:
                            split_w(it, first + 5)
                    elif kind == "pv" and c % NU in (1, 4):
                        split_ctx(it, c)
                    elif kind == "vt":
                        act.wait_ge(v_turned, it * 2 + (r // REP * 2 + n + 1))
                        f(v_hi[:, n * 4:(n + 1) * 4, :].rearrange("p k d -> p (k d)"),
                          work[:, place[(r, "vt", n)] % 2, :], ACT.Copy).then_inc(v_split_hi, 1)

            with act.Fori(0, B) as b:
                act.wait_ge(ln_step, b * LN_STEPS + (2 * NT + 1))
                f(rs[:, 1, 0:NT], rs[:, 0, 0:NT], ACT.Sqrt).then_inc(ln_root, 1)
                for t in range(NT):
                    act.wait_ge(ln_turned, b * NT + (t + 1))
                    f(xt_hi[:, :, t * P:(t + 1) * P],
                      score_ps[:, t % 4 // 2, t % 2 * D:(t % 2 + 1) * D].rearrange("p (c n) -> p c n", c=DC),
                      ACT.Copy).then_inc(ln_hi, 1)
                    if t == 3:
                        split_w(b * G, W_Q[0])
                split_w(b * G, W_K)
                for kind in ("q", "k"):
                    for n in range(2):
                        split_rope(b * G, -1, kind, n)
                    if kind == "q":
                        split_w(b * G, W_Q[1])
                work_through(b * G, 0, steps(0), None, START)
                with act.Fori(0, G - 1) as g:
                    for r in range(1, REP + 1):
                        work_through(b * G + g, r, steps(r), None, GROUP)
                for r in range(1, REP):
                    work_through(b * G + (G - 1), r, steps(r, False), None, END, False)
                split(b * G + (G - 1), UNITS_IT - 1)
                split_wo(b * G + (G - 1), REP - 1)
                work_through(b * G + (G - 1), REP, DRAIN, None, END)

            act.wait_ge(l2_step, 2 * TILES + 1)
            f(rs[:, 1, :], rs[:, 0, :], ACT.Sqrt).then_inc(l2_root, 1)

            def keep_logits(q):
                act.wait_ge(l2_logits_t, q + 1)
                if q > 1:
                    act.wait_ge(l2_logits, q - 1)
                f(logits_t[:, q % 2, :], work[0:E, 0, :], ACT.Copy).then_inc(l2_logits_kept, 1)

            for t in range(TILES):
                act.wait_ge(l2_turned, t + 1)
                q, i = divmod(t, 4)
                if q > 1 and i == 0:
                    act.wait_ge(l2_logits_t, q - 1)
                f(xn_t[:, q % 2, i, :], score_ps[:, t % 4 // 2, t % 2 * D:(t % 2 + 1) * D], ACT.Copy).then_inc(l2_copied, 1)
                if t % 4 == 1 and q:
                    keep_logits(q - 1)
            keep_logits(TILES // 4 - 1)
            act.wait_ge(route, SHIFTED)
            f(expo[:, :, :], expo[:, :, :], ACT.Exp).then_inc(route_exp, 1)
            def keep_rows(n, s):
                act.wait_ge(rows_turned, n * STEP + (s + 1))
                act.wait_ge(y_done, n * STEP + (s + 1))
                f(row_t[:, s % 2, :], ctx_ps[:, s % 2, :], ACT.Copy).then_inc(rows_copied, 1)

            with act.Fori(0, E // STEP) as n:
                for s in range(STEP):
                    keep_rows(n, s)
            act.wait_ge(route, EXPERTS_KNOWN)
            with act.If(act.value_load(overflow_i[0:1, 0:1], min_val=0, max_val=OVERFLOW_TILES) > 0):
                with act.Fori(0, OVERFLOW_TILES // STEP) as n:
                    for s in range(STEP):
                        keep_rows(n + E // STEP, s)

        @block.vector
        def _(dve):
            v = nc.vector
            for s, n in ((biased, 2), (ctx_split_lo, 2), (read_out, 2), (ln_lo, 4), (y_added, 2)):
                dve.sem_inc(s, n)
            v.memset(ones[:, :], 1.0).then_inc(ones_set, 1)

            def norm_stats(tile, tiles, stats, step, root, base, done):
                k = 0
                for t in range(tiles):
                    tile(t)
                k += tiles
                dve.wait_ge(step, base + k)
                dve.sem_inc(waited_dve, 1)
                for t in range(tiles):
                    v.bn_aggr(mean_var[:, t, :], stats[:, t, :]).then_inc(step, 1)
                k += tiles
                dve.wait_ge(step, base + k)
                a, root_a, y0, z = (rs[:, i, 0:tiles] for i in range(4))
                v.tensor_scalar(a, mean_var[:, 0:tiles, 1], LN_EPS, None, ALU.add).then_inc(step, 1)
                dve.wait_ge(root, done)
                v.reciprocal(y0, root_a).then_inc(step, 1)
                dve.wait_ge(step, base + (k + 2))
                v.tensor_tensor(z, y0, y0, ALU.mult).then_inc(step, 1)
                dve.wait_ge(step, base + (k + 3))
                v.scalar_tensor_tensor(out=z, in0=z, scalar=-0.5, in1=a, op0=ALU.mult, op1=ALU.mult).then_inc(step, 1)
                dve.wait_ge(step, base + (k + 4))
                v.scalar_tensor_tensor(out=y0, in0=z, scalar=1.5, in1=y0, op0=ALU.add, op1=ALU.mult).then_inc(step, 1)
                dve.wait_ge(step, base + (k + 5))

            def x_tile(b, t):
                return acc[:, bass.ds(b * NT + t, 1), :].rearrange("p a n -> p (a n)")

            def rotate(it, r, kind, n, jobs, place):
                pos = slice(n * 512, (n + 1) * 512)
                src = work[:, place[(r, kind, n)] % 2, :]
                w = (r + 1) // REP * W_IT + (W_K if kind == "k" else W_Q[(r + 1) % REP])
                dve.wait_ge(projected, it * (2 * W_IT) + (2 * w + n + 5))
                dve.wait_ge(rope_lo, it * ROPES_IT + (next_rope(r, kind, n) + 1))
                v.tensor_tensor(rope_a[:, n, :], src, cos_t[:, pos], ALU.mult)
                v.tensor_tensor(rope_b[0:64, n, :], src[64:128, :], sin_t[64:128, pos], ALU.mult)
                v.tensor_tensor(rope_b[64:128, n, :], src[0:64, :], sin_t[0:64, pos], ALU.mult).then_inc(read_out, 1)

            def bias(it, head_of_all, c):
                u, s = c % NU, c % P_SLOTS
                dve.wait_ge(scored, it * UNITS_IT + (c + 1))
                dve.wait_ge(pv_done, it * UNITS_IT + (c + 1))
                r_, u_ = divmod(c - P_SLOTS, NU)
                dve.wait_ge(p_added, it * (REP * ADDS) + ((r_ + 1) * ADDS + ADD_RANK[u_]))
                slope = slopes[:, bass.ds(head_of_all, 1)]
                if u in (2, 3):
                    a = 256 if u == 2 else 0
                    pairs = [(probs[:, s, 0:512], far[:, a:a + 512], score_ps[:, c % 2, 0:512]),
                             (probs[:, s, 512:1024], far[:, a + 128:a + 640], score_ps[:, c % 2, 512:1024])]
                elif u == 1:
                    halves = [near[:, :], probs[:, s, 0:512], score_ps[:, c % 2, 0:512]]
                    n_, p_, s_ = (z.rearrange("p (a c) -> p a c", a=2) for z in halves)
                    pairs = [(p_, n_[:, :, 0:256], s_)]
                else:
                    pairs = [(probs[:, s, :], near[:, :], score_ps[:, c % 2, :])]
                for dst, reach, src in pairs:
                    last = v.scalar_tensor_tensor(out=dst, in0=reach, scalar=slope, in1=src,
                                                  op0=ALU.mult, op1=ALU.add)
                last.then_inc(biased, 1)

            def split(it, c):
                s, w = c % P_SLOTS, WIDTH[c % NU]
                dve.wait_ge(p_split_hi, it * UNITS_IT + (c + 1))
                v.tensor_tensor(p_lo[:, s, 0:w], probs[:, s, 0:w], p_hi[:, s, 0:w].bitcast(F32), ALU.subtract
                                ).then_inc(p_split_lo, 1)

            def split_ctx(it, c):
                r, qc = c // NU, 0 if c % NU == 1 else 1
                dve.wait_ge(ctx_split_hi, (it * REP + r) * QC + (qc + 1))
                q = slice(qc * 512, (qc + 1) * 512)
                v.tensor_tensor(ctx_lo[:, q], ctx_ps[:, qc, :], ctx_hi[:, q].bitcast(F32), ALU.subtract
                                ).then_inc(ctx_split_lo, 1)

            def keep_v(it, r, n, place):
                w = r // REP * W_IT + W_V
                dve.wait_ge(projected, it * (2 * W_IT) + (2 * w + n + 5))
                dve.wait_ge(rope_sum, it * ROPES_IT + (next_rope(r, "q", n) + 1))
                v.tensor_copy(rope_b[:, n, :], work[:, place[(r, "v", n)] % 2, :]).then_inc(read_out, 1)

            def split_v(it, r, n, place):
                dve.wait_ge(v_split_hi, it * 2 + (r // REP * 2 + n + 1))
                rows = v_hi[:, n * 4:(n + 1) * 4, :].rearrange("p k d -> p (k d)")
                v.tensor_tensor(v_lo[:, n * 4:(n + 1) * 4, :].rearrange("p k d -> p (k d)"),
                                work[:, place[(r, "vt", n)] % 2, :], rows.bitcast(F32), ALU.subtract).then_inc(read_out, 1)

            def invert(it, r, place):
                dve.wait_ge(summed, it * REP + (r + 2))
                v.reciprocal(rinv[:, :], work[:, place[(r, "sum", 0)] % 2, 0:NT]).then_inc(read_out, 1)

            def add_out(it, r, t, b, jobs, place):
                i = place[(r, "out", t)]
                dve.wait_ge(out_done, (it * REP + r) * NT + (t + 1))
                if t == 0:
                    dve.wait_ge(read_out, jobs + (i + 2))
                else:
                    dve.wait_ge(read_out, jobs + (i - 5))
                v.scalar_tensor_tensor(out=x_tile(b, t), in0=work[:, i % 2, :], scalar=rinv[:, t:t + 1],
                                       in1=x_tile(b, t), op0=ALU.mult, op1=ALU.add).then_inc(read_out, 1)

            def work_through(it, head0, b, r, todo, jobs, place):
                whole = None
                unsplit = None
                for kind, n in todo:
                    c = r * NU + n
                    if unsplit is not None and kind in ("pv", "qk", "q", "k", "v", "vt"):
                        split(it, unsplit)
                        unsplit = None
                    if kind == "qk":
                        bias(it, head0 + r, c)
                        unsplit = c - 1 if c else None
                    elif kind in ("q", "k"):
                        rotate(it, r, kind, n, jobs, place)
                    elif kind == "v":
                        keep_v(it, r, n, place)
                    elif kind == "vt":
                        split_v(it, r, n, place)
                    elif kind == "sum":
                        invert(it, r, place)
                    elif kind == "out":
                        add_out(it, r, n, b, jobs, place)
                    if todo is DRAIN and kind == "out" and n:
                        second_stats(b, n - 1, jobs, place)
                    if whole is not None:
                        split_ctx(it, whole)
                        whole = None
                    if kind == "pv" and c % NU in (1, 4):
                        whole = c
                if unsplit is not None:
                    split(it, unsplit)

            def second_stats(b, t, jobs, place):
                dve.wait_ge(read_out, jobs + (place[(REP, "out", t)] + 3))
                v.bn_stats(stats2[:, bass.ds(b * NT + t, 1), :].rearrange("p a n -> p (a n)"), x_tile(b, t)
                           ).then_inc(l2_step, 1)

            with dve.Fori(0, B) as b:
                def first_stats(t):
                    if t % 2 == 0:
                        dve.wait_ge(x_in[t // 2], b * 16 + 16)
                    v.bn_stats(stats[:, t, :], x_tile(b, t)).then_inc(ln_step, 1)

                norm_stats(first_stats, NT, stats, ln_step, ln_root, b * LN_STEPS, b + 1)

                def split_turned(t):
                    dve.wait_ge(ln_hi, b * NT + (t + 1))
                    v.tensor_tensor(xt_lo[:, :, t * P:(t + 1) * P],
                                    score_ps[:, t % 4 // 2, t % 2 * D:(t % 2 + 1) * D].rearrange("p (c n) -> p c n", c=DC),
                                    xt_hi[:, :, t * P:(t + 1) * P].bitcast(F32), ALU.subtract).then_inc(ln_lo, 1)

                dve.wait_ge(p_added, b * (H * ADDS) + ADDS)
                for t in range(NT):
                    if t > 2:
                        split_turned(t - 3)
                    v.tensor_scalar(xnorm[:, t % 4, :], x_tile(b, t), mean_var[:, t, 0:1], rs[:, 2, t:t + 1],
                                    ALU.subtract, ALU.mult).then_inc(ln_normed, 1)
                for t in range(NT - 3, NT):
                    split_turned(t)
                dve.wait_ge(consts_in, 16 * CONSTS)
                for kind in ("q", "k"):
                    for n in range(2):
                        rotate(b * G, -1, kind, n, b * JOBS_BATCH, START)
                        dve.wait_ge(read_out, b * JOBS_BATCH + (START[(-1, kind, n)] + 3))
                        v.tensor_tensor(rope_a[:, n, :], rope_a[:, n, :], rope_b[:, n, :], ALU.add
                                        ).then_inc(rope_sum, 1)
                dve.wait_ge(bias_added, b * NT + NT)
                work_through(b * G, b * 0, b, 0, steps(0), b * JOBS_BATCH, START)
                with dve.Fori(0, G - 1) as g:
                    for r in range(1, REP + 1):
                        work_through(b * G + g, g * REP, b, r, steps(r), b * JOBS_BATCH + g * len(GROUP) + len(START),
                                     GROUP)
                end = b * JOBS_BATCH + (JOBS_BATCH - len(END))
                for r in range(1, REP):
                    work_through(b * G + (G - 1), b * 0 + (G - 1) * REP, b, r, steps(r, False), end, END)
                split(b * G + (G - 1), UNITS_IT - 1)
                work_through(b * G + (G - 1), None, b, REP, DRAIN, end, END)
                second_stats(b, NT - 1, end, END)

            def apply_mask(n, s):
                dve.wait_ge(mask_in[s], n * 16 + 16)
                v.tensor_tensor(mask_buffer[s], mask_buffer[s], weight_t[:, :], ALU.mult).then_inc(weighted, 1)

            def add_y(n, s):
                dve.wait_ge(y_done, n * STEP + (s + 3))
                dve.wait_ge(y_out[s % YS], n * (16 * STEP // YS) + 16 * (s // YS + 1))
                v.scalar_tensor_tensor(out=y[s % YS][:, :], in0=work[:, s % 2, :],
                                       scalar=slot_weight[:, bass.ds(n * STEP + s, 1)],
                                       in1=row[s % ROWS][:, D:2 * D], op0=ALU.mult, op1=ALU.add).then_inc(y_added, 1)

            dve.wait_ge(read_out, JOBS_DONE)
            norm_stats(lambda t: None, TILES, stats2, l2_step, l2_root, 0, 1)
            for t in range(TILES):
                v.tensor_scalar(xn[:, t, :], acc[:, t, :], mean_var[:, t, 0:1], rs[:, 2, t:t + 1],
                                ALU.subtract, ALU.mult).then_inc(l2_normed, 1)
            dve.wait_ge(consts2_in, 16 * CONSTS2)
            dve.wait_ge(weight_in, 32)
            v.tensor_scalar(weight_t[:, :], weight_t[:, :], 2.0, 1.0, ALU.mult, ALU.min).then_inc(weight_step, 1)
            dve.wait_ge(weight_step, 1)
            v.tensor_scalar(weight_t[:, :], weight_t[:, :], -1.0, ROUND, ALU.max, ALU.add).then_inc(weight_step, 1)
            dve.wait_ge(weight_step, 2)
            v.tensor_scalar(weight_t[:, :], weight_t[:, :], ROUND, None, ALU.subtract).then_inc(weight_step, 1)
            dve.wait_ge(weight_step, 3)
            w3 = weight_t[:, :].rearrange("p (c n) -> p c n", c=DC)
            v.tensor_tensor(w3, w3, scale_t[:, :].rearrange("p (a n) -> p a n", a=1).to_broadcast([P, DC, D]), ALU.mult
                            ).then_inc(weight_step, 1)
            dve.wait_ge(weight_step, 4)
            for s in range(STEP // 2):
                apply_mask(0, s)
            dve.wait_ge(l2_logits, TILES // 4)
            v.tensor_copy(logits[:, :, :].rearrange("p t e -> p (t e)"), work[:, 1, :]).then_inc(l2_kept, 1)
            dve.wait_ge(l2_kept, 1)

            count = [0]

            def step(ins):
                count[0] += 1
                ins.then_inc(route, 1)
                dve.wait_ge(route, count[0])

            def over_experts(ap):
                return ap.rearrange("p (t a) -> p t a", a=1).to_broadcast([P, TILES, E])

            step(v.tensor_reduce(top[:, :], logits[:, :, :], AX.X, ALU.max))
            step(v.tensor_tensor(expo[:, :, :], logits[:, :, :], over_experts(top[:, :]), ALU.subtract))
            assert count[0] == SHIFTED
            step(v.tensor_tensor(one_hot[:, :, :], logits[:, :, :], over_experts(top[:, :]), ALU.is_equal))
            step(v.scalar_tensor_tensor(out=rank[:, :, :], in0=one_hot[:, :, :], scalar=float(-E),
                                        in1=expert_ids[:, :, :], op0=ALU.mult, op1=ALU.add))
            step(v.tensor_reduce(first[:, :], rank[:, :, :], AX.X, ALU.min))
            step(v.tensor_scalar(first[:, :], first[:, :], float(E), None, ALU.add))
            step(v.tensor_tensor(one_hot[:, :, :], expert_ids[:, :, :], over_experts(first[:, :]), ALU.is_equal))
            assert count[0] == HOT_KNOWN
            dve.wait_ge(route_exp, 1)
            step(v.tensor_reduce(top_sum[:, :], expo[:, :, :], AX.X, ALU.add))
            step(v.reciprocal(tokens[:, :, 1], top_sum[:, :]))
            step(v.memset(before[:, 0, :], 0.0))
            dve.wait_ge(ranked, 2)
            for t in range(TILES):
                step(v.tensor_tensor(before[:, t + 1, :], score_ps[:, 1, t * E:(t + 1) * E], before[:, t, :], ALU.add))
            step(v.tensor_scalar(more_tiles_i[:, 0, :], before[:, TILES, :], -1.0, 0.0, ALU.add, ALU.max))
            step(v.tensor_scalar(more_tiles_i[:, 1, :], more_tiles_i[:, 0, :], 7, None, ALU.logical_shift_right))
            step(v.tensor_copy(more_tiles[:, 0, :], more_tiles_i[:, 1, :]))
            step(v.tensor_tensor_scan(more_tiles[:, 1, :], ones[:, 0:E], more_tiles[:, 0, :], 0.0, ALU.mult, ALU.add))
            step(v.tensor_tensor(more_tiles[:, 2, :], more_tiles[:, 1, :], more_tiles[:, 0, :], ALU.subtract))
            step(v.tensor_tensor(rank[:, :, :].rearrange("p t e -> p (t e)"), score_ps[:, 0, 0:512],
                                 before[:, 0:TILES, :].rearrange("p t e -> p (t e)"), ALU.add))
            step(v.tensor_tensor(rank[:, :, :], rank[:, :, :], one_hot[:, :, :], ALU.mult))
            number, overflow_slot, own_slot = (slot_parts[:, i, :] for i in range(3))
            step(v.tensor_reduce(number, rank[:, :, :], AX.X, ALU.add))
            step(v.tensor_tensor(rank[:, :, :], more_tiles[:, 2:3, :].to_broadcast([P, TILES, E]), one_hot[:, :, :],
                                 ALU.mult))
            step(v.tensor_reduce(overflow_slot, rank[:, :, :], AX.X, ALU.add))
            step(v.tensor_scalar(own_slot, first[:, :], float(P), None, ALU.mult))
            step(v.tensor_scalar(overflow_slot, overflow_slot, float(P), float(P * (E - 1)), ALU.mult, ALU.add))
            step(v.tensor_tensor(overflow_slot, overflow_slot, own_slot, ALU.subtract))
            step(v.scalar_tensor_tensor(out=overflow_slot, in0=number, scalar=float(P), in1=overflow_slot,
                                        op0=ALU.is_ge, op1=ALU.mult))
            step(v.tensor_tensor(own_slot, own_slot, number, ALU.add))
            step(v.tensor_tensor(slot_i[:, :], own_slot, overflow_slot, ALU.add))
            assert count[0] == SLOTS_KNOWN, count[0]
            step(v.tensor_tensor(tile_past[:, :, :], tile_ids[:, :, :],
                                 more_tiles[0:1, 1:2, :].to_broadcast([1, OVERFLOW_TILES, E]), ALU.is_ge))
            step(v.tensor_reduce(tile_expert[:, :], tile_past[:, :, :], AX.X, ALU.add))
            step(v.tensor_scalar(tile_expert_i[:, :], tile_expert[:, :], float(E - 1), None, ALU.min))
            step(v.tensor_copy(overflow_i[:, :], more_tiles[0:1, 1, E - 1:E]))
            assert count[0] == EXPERTS_KNOWN, count[0]
            dve.wait_ge(slots_turned, 2)
            v.tensor_copy(slot_tok_i[:, :], ctx_ps[:, 0, 0:SLOT_TILES]).then_inc(slots_copied, 1)
            v.tensor_copy(slot_weight[:, :], ctx_ps[:, 0, SLOT_TILES:2 * SLOT_TILES]).then_inc(slots_copied, 1)
            dve.wait_ge(slots_copied, 2)
            def expert_tiles(n, last):
                for s in range(STEP):
                    ahead = s + STEP // 2
                    if ahead < STEP:
                        apply_mask(n, ahead)
                    elif not last:
                        apply_mask(n + 1, ahead - STEP)
                    add_y(n, s)

            with dve.Fori(0, E // STEP - 1) as n:
                expert_tiles(n, False)
            expert_tiles(E // STEP - 1, True)
            with dve.If(dve.value_load(overflow_i[0:1, 0:1], min_val=0, max_val=OVERFLOW_TILES) > 0):
                with dve.Fori(0, OVERFLOW_TILES // STEP) as n:
                    for s in range(STEP):
                        apply_mask(n + E // STEP, s)
                        add_y(n + E // STEP, s)

        @block.gpsimd
        def _(pool):
            p = nc.gpsimd
            for s, n in ((rope_lo, 2), (p_added, ADDS), (w_split_lo, 1), (wo_split_lo, 1)):
                pool.sem_inc(s, n)

            def split_w(it, k):
                pool.wait_ge(w_split_hi, it * W_IT + (k + 1))
                p.tensor_tensor(w_lo[:, k % 2, :, :].rearrange("p c n -> p (c n)"), w_in[:, :],
                                w_hi[:, k % 2, :, :].rearrange("p c n -> p (c n)").bitcast(F32), ALU.subtract
                                ).then_inc(w_split_lo, 1)

            def split_wo(it, r):
                pool.wait_ge(wo_split_hi, it * REP + (r + 1))
                p.tensor_tensor(wo_lo[:, :], wo_in[:, :], wo_hi[:, :].bitcast(F32), ALU.subtract
                                ).then_inc(wo_split_lo, 1)

            def add_rope(it, r, kind, n, jobs, place):
                pool.wait_ge(read_out, jobs + (place[(r, kind, n)] + 3))
                p.tensor_tensor(rope_a[:, n, :], rope_a[:, n, :], rope_b[:, n, :], ALU.add).then_inc(rope_sum, 1)

            def split_rope(it, r, kind, n):
                pool.wait_ge(rope_hi, it * ROPES_IT + (next_rope(r, kind, n) + 1))
                hi, lo = (k_hi, k_lo) if kind == "k" else (q_hi[:, (r + 1) % 2], q_lo[:, (r + 1) % 2])
                pos = slice(n * 512, (n + 1) * 512)
                p.tensor_tensor(lo[:, pos], rope_a[:, n, :], hi[:, pos].bitcast(F32), ALU.subtract).then_inc(rope_lo, 1)

            def past_only(it, c):
                r, u = divmod(c, NU)
                s = c % P_SLOTS
                pool.wait_ge(exped, it * UNITS_IT + (c + 1))
                pool.sem_inc(waited_pool, 1)
                two = probs[:, s, 0:512 if u == 1 else 1024].rearrange("p (a c) -> p a c", a=2)[:, :, 0:P]
                last = p.affine_select(out=two, in_=two, compare_op=ALU.is_ge, fill=0.0, base=0,
                                       pattern=[[0, 2], [1, P]], channel_multiplier=-1)
                if u != 1:
                    one = probs[:, s, 896:1024]
                    last = p.affine_select(out=one, in_=one, compare_op=ALU.is_ge, fill=0.0, base=0,
                                           pattern=[[1, P]], channel_multiplier=-1)
                last.then_inc(masked, 1)
                pool.wait_ge(masked, (it * REP + r) * MASKS + MASK_RANK[u])

            def add_probs(it, r, k, q0, q1, a, b_=None):
                sums = psums[:, r % 2, q0:q1]
                pool.wait_ge(p_added, (it * REP + r) * ADDS + (ADDS + k - 1))
                if b_ is None:
                    p.tensor_tensor(sums, sums, a, ALU.add).then_inc(p_added, 1)
                else:
                    p.tensor_tensor(sums, a, b_, ALU.add).then_inc(p_added, 1)

            def sum_unit(it, r, u):
                def pr(unit, c0, c1):
                    return probs[:, (r * NU + unit) % P_SLOTS, c0:c1]

                if u == 0:
                    pool.wait_ge(summed, it * REP + (r + 1))
                    add_probs(it, r, 1, P, 512, pr(0, P, 512), pr(0, 512, 896))
                    pool.wait_ge(p_added, (it * REP + r) * ADDS + (ADDS + 1))
                    p.tensor_tensor(psums[:, r % 2, 0:P], pr(0, 0, P), ones[:, :], ALU.mult).then_inc(p_added, 1)
                    add_probs(it, r, 3, 384, 512, pr(0, 896, 1024))
                elif u == 1:
                    add_probs(it, r, 4, 256, 512, pr(1, 0, 256))
                elif u == 2:
                    pool.wait_ge(exped, it * UNITS_IT + (r * NU + 3))
                    add_probs(it, r, 5, 512, 1024, pr(2, 0, 512), pr(2, 512, 1024))
                    add_probs(it, r, 6, 768, 1024, pr(1, 256, 512))
                elif u == 3:
                    pool.wait_ge(exped, it * UNITS_IT + (r * NU + 4))
                    add_probs(it, r, 7, 512, 1024, pr(3, 0, 512))
                    add_probs(it, r, 8, 512, 1024, pr(3, 512, 1024))
                else:
                    add_probs(it, r, 9, 512, 1024, pr(4, 0, 512))
                    add_probs(it, r, 10, 640, 1024, pr(4, 512, 896))
                    add_probs(it, r, 11, 896, 1024, pr(4, 896, 1024))

            def work_through(it, r, todo, jobs, place, more=True):
                first = r // REP * W_IT
                for kind, n in todo:
                    if kind == "qk":
                        if n == NU - 1 and r == REP - 1 and more:
                            for i in range(2):
                                split_rope(it, r, "k", i)
                        if MASK_RANK[n]:
                            past_only(it, r * NU + n)
                        if n == 0 and r % REP == 0:
                            split_w(it, first + W_V)
                        if n == 1 and r:
                            split_wo(it, r - 1)
                        sum_unit(it, r, n)
                        if n in (1, 2) and (more or r < REP - 1):
                            split_rope(it, r, "q", n - 1)
                        if n == 2 and r % REP == 0:
                            split_w(it, first + 4)
                        elif n == 2 and more:
                            split_w(it, first + W_IT + r % REP - 1)
                        if n == 4 and r % REP == 0:
                            split_w(it, first + 5)
                    elif kind in ("q", "k"):
                        add_rope(it, r, kind, n, jobs, place)

            pool.wait_ge(consts_in, 16 * CONSTS)
            pool.wait_ge(ones_set, 1)
            with pool.Fori(0, B) as b:
                for t in range(NT):
                    if t == 4:
                        split_w(b * G, W_Q[0])
                    pool.wait_ge(ln_normed, b * NT + (t + 1))
                    tile = acc[:, bass.ds(b * NT + t, 1), :].rearrange("p a n -> p (a n)")
                    p.tensor_tensor(tile, tile, bo_t[:, :], ALU.add).then_inc(bias_added, 1)
                split_w(b * G, W_K)
                for kind in ("q", "k"):
                    for n in range(2):
                        split_rope(b * G, -1, kind, n)
                    if kind == "q":
                        split_w(b * G, W_Q[1])
                work_through(b * G, 0, steps(0), b * JOBS_BATCH, START)
                with pool.Fori(0, G - 1) as g:
                    for r in range(1, REP + 1):
                        work_through(b * G + g, r, steps(r), b * JOBS_BATCH + g * len(GROUP) + len(START), GROUP)
                for r in range(1, REP):
                    work_through(b * G + (G - 1), r, steps(r, False), b * JOBS_BATCH + (JOBS_BATCH - len(END)), END,
                                 False)
                split_wo(b * G + (G - 1), REP - 1)

            def store(s):
                p.indirect_dma_start(out_rows, bass.IndirectOffsetOnAxis(ap=out_idx[s][:, :], axis=0), y[s][:, :],
                                     None, bounds_check=B * T - 1, oob_is_err=False).then_inc(y_out[s], 16)

            pool.wait_ge(l2_logits, TILES // 4)
            for s in range(ROWS):
                p.memset(row[s], 0.0).then_inc(rows_cleared, 1)
            for s in range(YS):
                p.memset(y[s][:, :], 0.0).then_inc(rows_cleared, 1)
                p.memset(out_idx[s][:, :], NO_TOKEN).then_inc(rows_cleared, 1)
            pool.wait_ge(rows_cleared, ROWS + 2 * YS)
            for s in range(YS):
                store(s)
            pool.wait_ge(consts2_in, 16 * CONSTS2)
            pool.wait_ge(slots_cleared, 16)
            pool.wait_ge(route, SLOTS_KNOWN)
            for t in range(TILES):
                p.indirect_dma_start(slot_tokens_d, bass.IndirectOffsetOnAxis(ap=slot_i[:, t:t + 1], axis=0),
                                     tokens[:, t, :], None).then_inc(slots_written, 16)

            def set_index(idx, s, n, tile):
                p.tensor_copy(idx[s][:, :], slot_tok_i[:, bass.ds(n * STEP + tile, 1)]).then_inc(idx_set, 1)

            def gather(s):
                p.indirect_dma_start(row[s], None, rows_d, bass.IndirectOffsetOnAxis(ap=row_idx[s][:, :], axis=0),
                                     bounds_check=B * T - 1, oob_is_err=False).then_inc(row_in[s], 16)

            pool.wait_ge(slots_copied, 2)
            pool.wait_ge(x1_rows_out, 16 * B)
            pool.wait_ge(xn_rows_out, 16)
            for s in range(ROWS):
                set_index(row_idx, s, 0, s)
                pool.wait_ge(idx_set, s + 1)
                gather(s)

            def expert_tiles(n, last):
                for s in range(STEP):
                    i, j = s % ROWS, s % YS
                    more = s + ROWS < STEP or not last
                    pool.wait_ge(y_out[j], n * (16 * STEP // YS) + 16 * (s // YS + 1))
                    pool.sem_inc(waited_pool, 1)
                    set_index(out_idx, j, n, s)
                    if more:
                        pool.wait_ge(row_in[i], n * (16 * STEP // ROWS) + 16 * (s // ROWS + 1))
                        pool.sem_inc(waited_pool, 1)
                        set_index(row_idx, i, n, s + ROWS)
                    pool.wait_ge(idx_set, n * (2 * STEP) + (ROWS + 2 * s + 2 if more else STEP + s + 1))
                    pool.wait_ge(y_added, n * STEP + (s + 3))
                    pool.sem_inc(waited_pool, 1)
                    store(j)
                    if more:
                        gather(i)

            with pool.Fori(0, E // STEP - 1) as n:
                expert_tiles(n, False)
            expert_tiles(E // STEP - 1, True)
            with pool.If(pool.value_load(overflow_i[0:1, 0:1], min_val=0, max_val=OVERFLOW_TILES) > 0):
                with pool.Fori(0, OVERFLOW_TILES // STEP) as n:
                    for s in range(STEP):
                        i, j, m = s % ROWS, s % YS, n + E // STEP
                        pool.wait_ge(y_out[j], m * (16 * STEP // YS) + 16 * (s // YS + 1))
                        pool.wait_ge(row_in[i], m * (16 * STEP // ROWS) + 16 * (s // ROWS))
                        pool.wait_ge(y_added, m * STEP + (s + 3 - ROWS))
                        pool.sem_inc(waited_pool, 1)
                        set_index(out_idx, j, m, s)
                        set_index(row_idx, i, m, s)
                        pool.wait_ge(idx_set, m * (2 * STEP) + (2 * s + 2))
                        pool.sem_inc(waited_pool, 1)
                        gather(i)
                        pool.wait_ge(y_added, m * STEP + (s + 3))
                        pool.sem_inc(waited_pool, 1)
                        store(j)
                for s in range(YS):
                    pool.wait_ge(y_out[s], 16 * (SLOT_TILES // YS) + 16)
                for s in range(ROWS):
                    pool.wait_ge(row_in[s], 16 * (SLOT_TILES // ROWS))
            for s in range(YS):
                pool.wait_ge(y_out[s], 16 * (E // YS) + 16)
            for s in range(ROWS):
                pool.wait_ge(row_in[s], 16 * (E // ROWS))


def tables():
    inv_freq = (np.float32(1.0) / np.float32(ROPE_THETA) ** (np.arange(0, DH, 2, dtype=np.float32) / np.float32(DH)))
    angle = (np.arange(T, dtype=np.float32)[:, None] * inv_freq[None, :].astype(np.float32)).T
    cosines = np.concatenate([np.cos(angle)] * 2).astype(np.float32)
    sines = np.concatenate([np.sin(angle), -np.sin(angle)]).astype(np.float32)
    key = np.arange(P, dtype=np.float32)[:, None]
    near = np.concatenate([np.arange(w) for w in (512, 384, 128)]).astype(np.float32)[None, :] - key
    far = np.arange(P, 1024, dtype=np.float32)[None, :] - key
    slopes = 2.0 ** (-np.arange(1, H + 1, dtype=np.float32) * np.float32(8.0 / H))
    spread = np.ones((P, 1), np.float32)
    experts = np.arange(E, dtype=np.float32)
    return {
        "cosines": cosines, "sines": sines, "negslopes": -spread * slopes[None, :].astype(np.float32),
        "reach_near": near, "reach_far": far, "ident_in": np.eye(P, dtype=np.float32),
        "earlier_in": np.triu(np.ones((P, P), np.float32), 1),
        "expert_ids_in": np.tile(experts, (P, TILES, 1)),
        "tile_ids_in": np.repeat(np.arange(OVERFLOW_TILES, dtype=np.float32), E).reshape(1, OVERFLOW_TILES, E),
        "tokens_in": np.stack([np.arange(TILES) * P + np.arange(P)[:, None], np.zeros((P, TILES))], 2).astype(np.float32),
        "no_tokens_in": np.full((P, 2 * SLOT_TILES), NO_TOKEN, np.float32),
    }


def kernel(**inputs):
    from concourse import bacc
    from concourse.bass_utils import run_bass_kernel_spmd

    a = {k.split("_", 2)[2]: np.ascontiguousarray(v) for k, v in inputs.items()}
    halves = np.concatenate([np.arange(0, DH, 2), np.arange(1, DH, 2)])

    def by_head(w, order=slice(None)):
        return w.reshape(DC, P, -1, DH)[..., order].transpose(2, 1, 0, 3).reshape(-1, P, DC * DH)

    wq = by_head(a["Wq"], halves).reshape(G, REP, P, DC * DH)
    w = np.stack([wq[:, 0], by_head(a["Wk"], halves), wq[:, 1], by_head(a["Wv"]), wq[:, 2], wq[:, 3]], axis=1)
    arrays = {
        "x": a["hidden_states"],
        "w": w.reshape(G * W_IT, P, DC * DH),
        "wo": a["Wo"],
        "bo": np.tile(a["bo"], (P, 1)),
        "router": a["router_w"].T.reshape(DC, P, E).transpose(1, 0, 2),
        "weight": a["weight"].T.reshape(DC, P, D).transpose(1, 0, 2).reshape(P, DC * D),
        "scale": np.tile(a["scale"], (P, 1)),
        "masks": a["expert_masks"].transpose(0, 2, 1).reshape(E, DC, P, D).transpose(0, 2, 1, 3).reshape(E, P, DC * D),
        **tables(),
    }
    arrays = {f"{k}_dram": np.ascontiguousarray(v) for k, v in arrays.items()}
    nc = bacc.Bacc("TRN2", target_bir_lowering=False, num_devices=1)
    args = {k[:-5]: nc.dram_tensor(k, v.shape, mybir.dt.from_np(v.dtype), kind="ExternalInput").ap()
            for k, v in arrays.items()}
    args["rows_d"] = nc.dram_tensor("rows_scratch", (B * T, 2 * D), F32, kind="Internal").ap()
    args["slot_tokens_d"] = nc.dram_tensor("slot_tokens_scratch", (SLOT_TILES * P, 2), F32, kind="Internal").ap()
    args["out"] = nc.dram_tensor("out_dram", (B, T, D), F32, kind="ExternalOutput").ap()
    block_kernel(nc, **args)
    r = run_bass_kernel_spmd(nc, [arrays], core_ids=[0])
    return r.results[0]["out_dram"]
```
